# Optimizing a Trainium2 kernel written in Bass

```python
import numpy as np
import jax
import jax.numpy as jnp

def _softmax(x, axis=-1):
    return jax.nn.softmax(x, axis=axis)

def _gelu(x):
    return jax.nn.gelu(x, approximate=True)

def _silu(x):
    return jax.nn.silu(x)

def _sigmoid(x):
    return jax.nn.sigmoid(x)

def _layernorm(x, axis=-1, eps=1e-05):
    m = jnp.mean(x, axis=axis, keepdims=True)
    v = jnp.var(x, axis=axis, keepdims=True)
    return (x - m) / jnp.sqrt(v + eps)

def _scatter_add(tgt, idx, src, axis=0):
    return tgt.at[idx].add(src)

def _segment_sum(src, seg, n):
    return jax.ops.segment_sum(src, seg, n)
kernel_name = 'mk_gnn_resnorm_d4_gnn_r32_305566'

def setup_inputs(seed: int=0):
    np.random.seed(seed)
    _w = jnp.asarray

    def _rec_inputs():
        import jax
        import jax.numpy as jnp
        _gk = jax.random.key(seed)
        x = -0.000202 + 1 * jax.random.normal(jax.random.fold_in(_gk, 1), (3125, 64), jnp.float32)
        _s = jax.random.randint(jax.random.fold_in(_gk, 2), (25000,), 0, 3125, jnp.int32)
        _d = jax.random.randint(jax.random.fold_in(_gk, 3), (25000,), 0, 3125, jnp.int32)
        _loop = jnp.arange(3125, dtype=jnp.int32)
        src = jnp.concatenate([_s, _d, _loop])
        dst = jnp.concatenate([_d, _s, _loop])
        _o = jnp.argsort(dst, stable=True)
        src = src[_o]
        dst = dst[_o]
        edge_type_65 = jax.random.randint(jax.random.fold_in(_gk, 13), (53125,), 0, 65, jnp.int32)
        edge_type_8 = jax.random.randint(jax.random.fold_in(_gk, 14), (53125,), 0, 8, jnp.int32)
        edge_weight = jax.random.uniform(jax.random.fold_in(_gk, 15), (53125,), jnp.float32, 0.0, 0.999998)
        return (x, src, dst, edge_type_65, edge_type_8, edge_weight)
    x, src, dst, edge_type_65, edge_type_8, edge_weight = _rec_inputs()

    def _L0_gnn_setup():
        import jax, jax.numpy as jnp
        import numpy as np

        def gin_layer(x, src, dst, ew, w1, b1, w2, b2):
            msg = x[src] * ew[:, None]
            agg = jax.ops.segment_sum(msg, dst, num_segments=x.shape[0])
            h = agg + x
            h = jax.nn.relu(h @ w1 + b1)
            return h @ w2 + b2
        key = jax.random.key(seed)
        ks = jax.random.split(key, 16)
        N, E, D = (3125, 31250, 64)
        x = jax.random.normal(ks[0], (N, D), dtype=jnp.float32)
        edge_index = jax.random.randint(ks[1], (2, E), 0, N)
        edge_weight = jax.random.uniform(ks[2], (E,), dtype=jnp.float32)

        def lin(k, fi, fo):
            return jax.random.normal(k, (fi, fo), dtype=jnp.float32) * (1.0 / np.sqrt(fi))
        return {'x': x, 'edge_index': edge_index, 'edge_weight': edge_weight, 'w11': lin(ks[3], 64, 64), 'b11': jnp.zeros(64, jnp.float32), 'w12': lin(ks[4], 64, 64), 'b12': jnp.zeros(64, jnp.float32), 'w21': lin(ks[5], 64, 128), 'b21': jnp.zeros(128, jnp.float32), 'w22': lin(ks[6], 128, 64), 'b22': jnp.zeros(64, jnp.float32), 'w31': lin(ks[7], 64, 64), 'b31': jnp.zeros(64, jnp.float32), 'w32': lin(ks[8], 64, 64), 'b32': jnp.zeros(64, jnp.float32)}
    _L0_gnn_all = _L0_gnn_setup()
    _L0_gnn_in = {k: v for k, v in _L0_gnn_all.items() if k in ('w11', 'b11', 'w12', 'b12', 'w21', 'b21', 'w22', 'b22', 'w31', 'b31', 'w32', 'b32')}
    del _L0_gnn_all

    def _L1_gnn_setup():
        import jax, jax.numpy as jnp
        import numpy as np
        N, E, D, R, L = (50000, 18750, 64, 65, 2)

        def _rgcn_conv(x, src, dst, edge_type, W_r, W_root, b):
            n, d = x.shape
            r = W_r.shape[0]
            seg = dst * r + edge_type
            msg = x[src]
            agg = jax.ops.segment_sum(msg, seg, num_segments=n * r).reshape(n, r, d)
            cnt = jax.ops.segment_sum(jnp.ones((msg.shape[0],), x.dtype), seg, num_segments=n * r).reshape(n, r, 1)
            mean = agg / jnp.maximum(cnt, 1.0)
            out = jnp.einsum('nrd,rdk->nk', mean, W_r)
            return out + x @ W_root + b
        key = jax.random.key(seed)
        ks = jax.random.split(key, 10)
        x = jax.random.normal(ks[0], (N, D), dtype=jnp.float32)
        edge_index = jax.random.randint(ks[1], (2, E), 0, N, dtype=jnp.int64)
        edge_type = jax.random.randint(ks[2], (E,), 0, R, dtype=jnp.int64)
        s = 1.0 / np.sqrt(D)
        W = jax.random.normal(ks[3], (L, R, D, D), dtype=jnp.float32) * s
        root = jax.random.normal(ks[4], (L, D, D), dtype=jnp.float32) * s
        bias = jax.random.normal(ks[5], (L, D), dtype=jnp.float32) * 0.01
        res_W = jax.random.normal(ks[6], (L, D, D), dtype=jnp.float32) * s
        res_b = jax.random.normal(ks[7], (L, D), dtype=jnp.float32) * 0.01
        return {'x': x, 'edge_index': edge_index, 'edge_type': edge_type, 'W': W, 'root': root, 'bias': bias, 'res_W': res_W, 'res_b': res_b}
    _L1_gnn_all = _L1_gnn_setup()
    _L1_gnn_in = {k: v for k, v in _L1_gnn_all.items() if k in ('W', 'root', 'bias', 'res_W', 'res_b')}
    del _L1_gnn_all

    def _L2_gnn_setup():
        import jax, jax.numpy as jnp
        import numpy as np
        N = 50000
        E = 25000
        D_IN = 64
        D_OUT = 64
        key = jax.random.key(seed)
        k1, k2, k3 = jax.random.split(key, 3)
        x = jax.random.normal(k1, (N, D_IN), dtype=jnp.float32)
        edge_index = jax.random.randint(k2, (2, E), 0, N, dtype=jnp.int32)
        W = jax.random.normal(k3, (D_OUT, D_IN), dtype=jnp.float32) * 0.05
        b = jnp.zeros((D_OUT,), dtype=jnp.float32)
        prelu_a = jnp.full((1,), 0.25, dtype=jnp.float32)
        return {'x': x, 'edge_index': edge_index, 'W': W, 'b': b, 'prelu_a': prelu_a}
    _L2_gnn_all = _L2_gnn_setup()
    _L2_gnn_in = {k: v for k, v in _L2_gnn_all.items() if k in ('W', 'b', 'prelu_a')}
    del _L2_gnn_all

    def _L3_gnn_setup():
        import jax, jax.numpy as jnp
        import numpy as np
        N_NODES = 50000
        N_EDGES = 25000
        IN_DIM = 64
        OUT_DIM = 64
        NUM_RELS = 8
        key = jax.random.key(seed)
        ks = jax.random.split(key, 9)
        node_features = jax.random.normal(ks[0], (N_NODES, IN_DIM), dtype=jnp.float32)
        src = jax.random.randint(ks[1], (N_EDGES,), 0, N_NODES)
        dst = jax.random.randint(ks[2], (N_EDGES,), 0, N_NODES)
        etypes = jax.random.randint(ks[3], (N_EDGES,), 0, NUM_RELS)
        s_in = 1.0 / np.sqrt(IN_DIM).astype(np.float32)
        s_out = 1.0 / np.sqrt(OUT_DIM).astype(np.float32)
        W_enc = jax.random.normal(ks[4], (IN_DIM, OUT_DIM), dtype=jnp.float32) * s_in
        b_enc = jnp.zeros((OUT_DIM,), dtype=jnp.float32)
        W_rel = jax.random.normal(ks[5], (NUM_RELS, OUT_DIM, OUT_DIM), dtype=jnp.float32) * s_out
        W_self = jax.random.normal(ks[6], (OUT_DIM, OUT_DIM), dtype=jnp.float32) * s_out
        bias = jnp.zeros((OUT_DIM,), dtype=jnp.float32)
        return {'node_features': node_features, 'src': src, 'dst': dst, 'etypes': etypes, 'W_enc': W_enc, 'b_enc': b_enc, 'W_rel': W_rel, 'W_self': W_self, 'bias': bias}
    _L3_gnn_all = _L3_gnn_setup()
    _L3_gnn_in = {k: v for k, v in _L3_gnn_all.items() if k in ('W_enc', 'b_enc', 'W_rel', 'W_self', 'bias')}
    del _L3_gnn_all
    return {'x': x, 'src': src, 'dst': dst, 'edge_type_65': edge_type_65, 'edge_type_8': edge_type_8, 'edge_weight': edge_weight, 'L0_gnn_w11': _L0_gnn_in['w11'], 'L0_gnn_b11': _L0_gnn_in['b11'], 'L0_gnn_w12': _L0_gnn_in['w12'], 'L0_gnn_b12': _L0_gnn_in['b12'], 'L0_gnn_w21': _L0_gnn_in['w21'], 'L0_gnn_b21': _L0_gnn_in['b21'], 'L0_gnn_w22': _L0_gnn_in['w22'], 'L0_gnn_b22': _L0_gnn_in['b22'], 'L0_gnn_w31': _L0_gnn_in['w31'], 'L0_gnn_b31': _L0_gnn_in['b31'], 'L0_gnn_w32': _L0_gnn_in['w32'], 'L0_gnn_b32': _L0_gnn_in['b32'], 'L1_gnn_W': _L1_gnn_in['W'], 'L1_gnn_root': _L1_gnn_in['root'], 'L1_gnn_bias': _L1_gnn_in['bias'], 'L1_gnn_res_W': _L1_gnn_in['res_W'], 'L1_gnn_res_b': _L1_gnn_in['res_b'], 'L2_gnn_W': _L2_gnn_in['W'], 'L2_gnn_b': _L2_gnn_in['b'], 'L2_gnn_prelu_a': _L2_gnn_in['prelu_a'], 'L3_gnn_W_enc': _L3_gnn_in['W_enc'], 'L3_gnn_b_enc': _L3_gnn_in['b_enc'], 'L3_gnn_W_rel': _L3_gnn_in['W_rel'], 'L3_gnn_W_self': _L3_gnn_in['W_self'], 'L3_gnn_bias': _L3_gnn_in['bias']}

def reference(x, src, dst, edge_type_65, edge_type_8, edge_weight, L0_gnn_w11, L0_gnn_b11, L0_gnn_w12, L0_gnn_b12, L0_gnn_w21, L0_gnn_b21, L0_gnn_w22, L0_gnn_b22, L0_gnn_w31, L0_gnn_b31, L0_gnn_w32, L0_gnn_b32, L1_gnn_W, L1_gnn_root, L1_gnn_bias, L1_gnn_res_W, L1_gnn_res_b, L2_gnn_W, L2_gnn_b, L2_gnn_prelu_a, L3_gnn_W_enc, L3_gnn_b_enc, L3_gnn_W_rel, L3_gnn_W_self, L3_gnn_bias):
    import jax
    import jax.numpy as jnp

    def _L0_gnn_ref(x, edge_index, edge_weight, w11, b11, w12, b12, w21, b21, w22, b22, w31, b31, w32, b32):
        import jax, jax.numpy as jnp
        import numpy as np

        def gin_layer(x, src, dst, ew, w1, b1, w2, b2):
            msg = x[src] * ew[:, None]
            agg = jax.ops.segment_sum(msg, dst, num_segments=x.shape[0])
            h = agg + x
            h = jax.nn.relu(h @ w1 + b1)
            return h @ w2 + b2
        src, dst = (edge_index[0], edge_index[1])
        h = gin_layer(x, src, dst, edge_weight, w11, b11, w12, b12)
        h = jax.nn.relu(h)
        h = gin_layer(h, src, dst, edge_weight, w21, b21, w22, b22)
        h = jax.nn.relu(h)
        h = gin_layer(h, src, dst, edge_weight, w31, b31, w32, b32)
        return h

    def _L1_gnn_ref(x, edge_index, edge_type, W, root, bias, res_W, res_b):
        import jax, jax.numpy as jnp
        import numpy as np
        N, E, D, R, L = (50000, 18750, 64, 65, 2)

        def _rgcn_conv(x, src, dst, edge_type, W_r, W_root, b):
            n, d = x.shape
            r = W_r.shape[0]
            seg = dst * r + edge_type
            msg = x[src]
            agg = jax.ops.segment_sum(msg, seg, num_segments=n * r).reshape(n, r, d)
            cnt = jax.ops.segment_sum(jnp.ones((msg.shape[0],), x.dtype), seg, num_segments=n * r).reshape(n, r, 1)
            mean = agg / jnp.maximum(cnt, 1.0)
            out = jnp.einsum('nrd,rdk->nk', mean, W_r)
            return out + x @ W_root + b
        src, dst = (edge_index[0], edge_index[1])
        h = x
        for l in range(W.shape[0]):
            conv = _rgcn_conv(h, src, dst, edge_type, W[l], root[l], bias[l])
            conv = jax.nn.relu(conv)
            res = jax.nn.relu(h @ res_W[l] + res_b[l])
            h = conv + res
        return h

    def _L2_gnn_ref(x, edge_index, W, b, prelu_a):
        import jax, jax.numpy as jnp
        import numpy as np
        N = 50000
        E = 25000
        D_IN = 64
        D_OUT = 64
        n = x.shape[0]
        row, col = (edge_index[0], edge_index[1])
        loop = jnp.arange(n, dtype=edge_index.dtype)
        row = jnp.concatenate([row, loop])
        col = jnp.concatenate([col, loop])
        ones = jnp.ones(row.shape[0], dtype=x.dtype)
        deg = jax.ops.segment_sum(ones, col, num_segments=n)
        dinv = jnp.where(deg > 0, jax.lax.rsqrt(deg), 0.0)
        norm = dinv[row] * dinv[col]
        h = x @ W.T
        msg = h[row] * norm[:, None]
        out = jax.ops.segment_sum(msg, col, num_segments=n) + b
        return jnp.where(out >= 0, out, prelu_a * out)

    def _L3_gnn_ref(node_features, src, dst, etypes, W_enc, b_enc, W_rel, W_self, bias):
        import jax, jax.numpy as jnp
        import numpy as np
        N_NODES = 50000
        N_EDGES = 25000
        IN_DIM = 64
        OUT_DIM = 64
        NUM_RELS = 8
        n_nodes = node_features.shape[0]
        h0 = jax.nn.relu(node_features @ W_enc + b_enc)
        hW = jnp.einsum('nd,rdo->rno', h0, W_rel)
        msgs = hW[etypes, src]
        agg = jax.ops.segment_sum(msgs, dst, num_segments=n_nodes)
        h1 = jax.nn.relu(agg + h0 @ W_self + bias)
        return h0 + h1
    edge_index = jnp.stack([src, dst])
    x = _layernorm(x + _L0_gnn_ref(x, edge_index, edge_weight, L0_gnn_w11, L0_gnn_b11, L0_gnn_w12, L0_gnn_b12, L0_gnn_w21, L0_gnn_b21, L0_gnn_w22, L0_gnn_b22, L0_gnn_w31, L0_gnn_b31, L0_gnn_w32, L0_gnn_b32), axis=-1)
    x = _layernorm(x + _L1_gnn_ref(x, edge_index, edge_type_65, L1_gnn_W, L1_gnn_root, L1_gnn_bias, L1_gnn_res_W, L1_gnn_res_b), axis=-1)
    x = _layernorm(x + _L2_gnn_ref(x, edge_index, L2_gnn_W, L2_gnn_b, L2_gnn_prelu_a), axis=-1)
    x = _layernorm(x + _L3_gnn_ref(x, src, dst, edge_type_8, L3_gnn_W_enc, L3_gnn_b_enc, L3_gnn_W_rel, L3_gnn_W_self, L3_gnn_bias), axis=-1)
    return x

_drawn_inputs = setup_inputs


def setup_inputs(seed=0):
    import zlib

    import numpy as np

    out = dict(_drawn_inputs(seed))
    spreads = {'L0_gnn_b11': (0.0, 0.1),
     'L0_gnn_b12': (0.0, 0.1),
     'L0_gnn_b21': (0.0, 0.8),
     'L0_gnn_b22': (0.0, 0.482),
     'L0_gnn_b31': (0.0, 2.0),
     'L0_gnn_b32': (0.0, 2.0),
     'L2_gnn_b': (0.0, 0.1),
     'L3_gnn_b_enc': (0.0, 0.1),
     'L3_gnn_bias': (0.0, 0.275)}
    factors = {'L1_gnn_bias': 8.0, 'L1_gnn_res_b': 8.0}
    for name, (base, spread) in spreads.items():
        noise = np.random.default_rng([zlib.crc32(name.encode()), seed]).standard_normal(out[name].shape)
        drawn = base * np.exp(spread * noise) if base else spread * noise
        out[name] = jnp.asarray(drawn.astype(out[name].dtype))
    for name, factor in factors.items():
        out[name] = (out[name] * factor).astype(out[name].dtype)
    return out
```

```python
from contextlib import ExitStack

import concourse.bass as bass
from concourse import mybir

F32 = mybir.dt.float32
BF16 = mybir.dt.bfloat16
I32 = mybir.dt.int32
ALU = mybir.AluOpType
ACT = mybir.ActivationFunctionType
AX = mybir.AxisListType

D = 64
TILE = 16
GROUP = 128 * TILE
WIN = 256
BLK = 120
SHIFT = 64
NOWHERE = 10000.0
EPS = 1e-5
PASSES = 7
GIN, RGCN, GCN, REL = (0, 1, 2), (3, 4), 5, 6


def bass_gnn(nc, A, out, scratch):
    N = A["x"].shape[0]
    E = A["src"].shape[0]
    R65 = A["L1_gnn_W"].shape[1]
    R8 = A["L3_gnn_W_rel"].shape[0]
    NG = -(-E // GROUP)
    NB = -(-(N + SHIFT) // BLK)
    SLOTS = -(-(N + SHIFT) // WIN) * WIN
    SWEEPS = SLOTS // WIN
    LAST = E - (NG - 1) * GROUP
    HEAD = BLK - SHIFT
    TAIL = N + SHIFT - (NB - 1) * BLK
    TW = R65 * D
    CHUNKS = [(c, min(512, TW - c)) for c in range(0, TW, 512)]
    assert NG % 2 == 0 and NB == NG + 1 and BLK * (NG - 1) + WIN <= SLOTS
    PAIRS = NG // 2

    with ExitStack() as ctx:
        def sb(name, shape, dt=F32):
            return ctx.enter_context(nc.sbuf_tensor(name, shape, dt))

        def pb(name):
            return ctx.enter_context(nc.psum_tensor(name, [128, 512], F32))

        sems = {}

        def sem(*name):
            key = "_".join(str(x) for x in name)
            if key not in sems:
                sems[key] = ctx.enter_context(nc.semaphore("s_" + key))
            return sems[key]

        src_i = sb("src_i", [128, NG * TILE], I32)
        dst_i = sb("dst_i", [128, NG * TILE], I32)
        t65_i = sb("t65_i", [128, NG * TILE], I32)
        t8_i = sb("t8_i", [128, NG * TILE], I32)
        edge_w = sb("edge_w", [128, NG * TILE])
        row_slot = sb("row_slot", [128, NG * TILE], I32)
        row_65 = sb("row_65", [128, NG * TILE], I32)
        row_8 = sb("row_8", [128, NG * TILE], I32)
        slot_f = sb("slot_f", [128, NG * TILE])
        t65_f = sb("t65_f", [128, NG * TILE])
        mean_w = sb("mean_w", [128, NG * TILE])
        scratch_f = sb("scratch_f", [128, NG * TILE])
        last_mask = sb("last_mask", [128, TILE])
        iota_win = sb("iota_win", [128, WIN])
        iota_win_bf = sb("iota_win_bf", [128, WIN], BF16)
        iota_type = sb("iota_type", [128, TILE * R65], BF16)
        group_base = sb("group_base", [128, NG])
        sweep_base = sb("sweep_base", [128, SWEEPS])
        ident = sb("ident", [128, 128])
        ones = sb("ones", [128, 1])
        zeros = sb("zeros", [D, BLK])
        eps = sb("eps", [128, 1])
        worst = sb("worst", [128, 2])
        flag_f = sb("flag_f", [128, 1])
        flag_i = sb("flag_i", [1, 1], I32)
        rows_now = sb("rows_now", [128, 2, TILE], I32)
        msgs = sb("msgs", [128, 2, TILE, D])
        hot = sb("hot", [128, 2, TILE, WIN])
        rel_now = sb("rel_now", [128, TILE])
        w_now = sb("w_now", [128, TILE])
        hot_bf = sb("hot_bf", [128, TILE, WIN], BF16)
        type_hot_bf = sb("type_hot_bf", [128, TILE, R65], BF16)
        type_hot = sb("type_hot", [128, TILE, R65])
        type_hot_t = sb("type_hot_t", [R65, TILE, 128])
        inv_now = sb("inv_now", [R65, WIN])
        mean_now = sb("mean_now", [128, TILE])
        junk = sb("junk", [128, 4, WIN])
        acc = sb("acc", [D, SLOTS])
        counts = sb("counts", [R65, SLOTS])
        x_fm = sb("x_fm", [D, NB * BLK])
        h_fm = sb("h_fm", [D, NB * BLK])
        x_nm = sb("x_nm", [BLK, NB, D])
        hws_nm = sb("hws_nm", [BLK, NB, D])
        dinv = sb("dinv", [BLK, NB])
        in_blk = sb("in_blk", [D, BLK])
        hid_blk = sb("hid_blk", [128, BLK])
        out_blk = sb("out_blk", [D, BLK])
        res_blk = sb("res_blk", [D, BLK])
        y_blk = sb("y_blk", [D, BLK])
        xblk = sb("xblk", [D, BLK])
        nm_blk = sb("nm_blk", [BLK, D])
        z_blk = sb("z_blk", [BLK, D])
        y_nm = sb("y_nm", [BLK, D])
        neg_nm = sb("neg_nm", [BLK, D])
        stats = sb("stats", [BLK, 6])
        mean_var = sb("mean_var", [BLK, 2])
        std = sb("std", [BLK, 1])
        rstd = sb("rstd", [BLK, 1])
        table_blk = sb("table_blk", [BLK, TW])
        w65 = sb("w65", [D, TW])
        w8 = sb("w8", [D, R8 * D])
        gin_w1 = [sb(f"gin_w1_{p}", [D, A[f"L0_gnn_w{p + 1}1"].shape[1]]) for p in GIN]
        gin_w2 = [sb(f"gin_w2_{p}", [A[f"L0_gnn_w{p + 1}2"].shape[0], D]) for p in GIN]
        gin_b1 = [sb(f"gin_b1_{p}", [A[f"L0_gnn_w{p + 1}1"].shape[1], 1]) for p in GIN]
        gin_b2 = [sb(f"gin_b2_{p}", [D, 1]) for p in GIN]
        root = [sb(f"root{n}", [D, D]) for n in range(2)]
        res_w = [sb(f"res_w{n}", [D, D]) for n in range(2)]
        rg_b = [sb(f"rg_b{n}", [D, 1]) for n in range(2)]
        res_b = [sb(f"res_b{n}", [D, 1]) for n in range(2)]
        gcn_w = sb("gcn_w", [D, D])
        gcn_wt = sb("gcn_wt", [D, D])
        gcn_b = sb("gcn_b", [BLK, D])
        prelu_a = sb("prelu_a", [BLK, 1])
        w_enc = sb("w_enc", [D, D])
        b_enc = sb("b_enc", [D, 1])
        w_self = sb("w_self", [D, D])
        rel_b = sb("rel_b", [D, 1])
        sum_ps = [pb("sum_ps0"), pb("sum_ps1")]
        aux_ps = [pb("aux_ps0"), pb("aux_ps1")]
        post_ps = pb("post_ps")
        tab_ps = [pb(f"tab_ps{n}") for n in range(3)]
        fm_a = post_ps[:, 0:BLK]
        fm_b = post_ps[:, 128:128 + BLK]
        nm_ps = post_ps[0:BLK, 256:256 + D]

        gathers = [(A["x"], src_i), (scratch["h1"], row_slot), (scratch["h2"], row_slot),
                   (scratch["t65a"], row_65), (scratch["t65b"], row_65), (scratch["hw"], row_slot),
                   (scratch["t8"], row_8)]
        edge_scale = [edge_w, edge_w, edge_w, mean_w, mean_w, None, None]

        per_step = {"rows_staged": 1, "summed": 1, "hot_done": 1, "added": 1}
        per_block = {
            "in_done": (range(PASSES), 1), "stored": (range(PASSES), 16), "cleared": (range(PASSES), 1),
            "hidden": (GIN, 1), "hidden_relu": (GIN, 1), "gin_out": (GIN, 1),
            "out_done": ((0, 1, 2, 5), 1), "out_turned": ((0, 1), 1), "rows_ready": ((0, 1, 4, 5, 6), 1),
            "y_done": ((2, 4, 5, 6), 1), "y_turned": ((2, 4, 6), 1), "stats": ((2, 4, 5, 6), 1),
            "moments": ((2, 4, 5, 6), 1), "std_done": ((2, 4, 5, 6), 1), "rstd": ((2, 4, 5, 6), 1),
            "z_done": ((2, 4, 5), 1), "z_turned": ((2, 4, 5), 1), "xblk_done": ((2, 3, 4, 5), 1),
            "conv_mult": ((3, 4, 6), 1), "conv_sum": ((3, 4, 6), 1), "conv_relu": ((3, 4, 6), 1),
            "gcn_mult": ((4,), 1), "encoded": ((5,), 1), "sum_turned": ((5,), 1),
            "tab_act": ((2, 3), 5), "tab_dve": ((2, 3), 4)}

        def before(name, p, general):
            steps = SWEEPS * NG if general else NG
            if name in per_step:
                return p * steps * per_step[name]
            if name == "staged":
                return sum(steps * (1 if edge_scale[q] is None else 2) for q in range(p))
            if name == "tab_mult":
                return NB * sum({2: 9, 3: 9, 5: 1}.get(q, 0) for q in range(p))
            users, n = per_block[name]
            return NB * n * sum(q < p for q in users)

        def load_edges(eng, tile, src):
            full = (NG - 1) * GROUP
            t = tile[:, :].rearrange("p (g j) -> p g j", j=TILE)
            eng.dma_start(t[:, 0:NG - 1, :], src[0:full].rearrange("(g p j) -> p g j", p=128, j=TILE))\
               .then_inc(sem("edges_in"), 16)
            rows, rest = LAST // TILE, LAST % TILE
            eng.dma_start(t[0:rows, NG - 1, :],
                          src[full:full + rows * TILE].rearrange("(p j) -> p j", j=TILE))\
               .then_inc(sem("edges_in"), 16)
            eng.dma_start(t[rows:rows + 1, NG - 1, 0:rest],
                          src[full + rows * TILE:E].rearrange("(a j) -> a j", a=1))\
               .then_inc(sem("edges_in"), 16)

        small = [(gcn_w, A["L2_gnn_W"]), (w_enc, A["L3_gnn_W_enc"]), (w_self, A["L3_gnn_W_self"])]
        cols = [(b_enc, A["L3_gnn_b_enc"]), (rel_b, A["L3_gnn_bias"])]
        for p in GIN:
            small += [(gin_w1[p], A[f"L0_gnn_w{p + 1}1"]), (gin_w2[p], A[f"L0_gnn_w{p + 1}2"])]
            cols += [(gin_b1[p], A[f"L0_gnn_b{p + 1}1"]), (gin_b2[p], A[f"L0_gnn_b{p + 1}2"])]
        for n in range(2):
            small += [(root[n], A["L1_gnn_root"][n]), (res_w[n], A["L1_gnn_res_W"][n])]
            cols += [(rg_b[n], A["L1_gnn_bias"][n]), (res_b[n], A["L1_gnn_res_b"][n])]
        WEIGHTS = 16 * (len(small) + len(cols) + 2 + 1)

        def cols_of(tile, b):
            return tile[:, b * BLK:(b + 1) * BLK] if isinstance(b, int) else tile[:, bass.ds(b * BLK, BLK)]

        def col16(tile, g):
            return tile[:, g * TILE:(g + 1) * TILE] if isinstance(g, int) else tile[:, bass.ds(g * TILE, TILE)]

        def at(tile, n, w=1):
            return tile[:, n:n + w] if isinstance(n, int) else tile[:, bass.ds(n, w)]

        def nm_at(tile, b):
            return tile[:, b, :] if isinstance(b, int) else \
                tile[:, bass.ds(b, 1), :].rearrange("p a d -> p (a d)")

        def schedule(eng, general, step, finish, extra=None, finish_first=False):
            def turn(s, g, k, u, n, b):
                if finish_first and b is not None:
                    finish(b, b + 1)
                step(s, g, k, u, n)
                if not finish_first and b is not None:
                    finish(b, b + 1)
                if extra:
                    extra(s, g, k, u)

            if general:
                with eng.Fori(0, SWEEPS) as k:
                    with eng.Fori(0, PAIRS) as i:
                        for u in range(2):
                            turn(k * NG + 2 * i + u, 2 * i + u, k, u, k * PAIRS + i, None)
                finish(0, SWEEPS * NG)
                with eng.Fori(1, NB) as b:
                    finish(b, SWEEPS * NG)
                return
            turn(0, 0, None, 0, 0, None)
            turn(1, 1, None, 1, 0, 0)
            with eng.Fori(1, PAIRS) as i:
                for u in range(2):
                    s = 2 * i + u
                    turn(s, s, None, u, i, s - 1)
            step(NG, None, None, None, None)
            finish(NG - 1, NG)
            finish(NB - 1, NG)

        def by_branch(eng, run):
            eng.wait_ge(sem("flag_ready"), 1)
            general = eng.value_load(flag_i[0:1, 0:1], min_val=0, max_val=1)
            with eng.If(general == 0):
                run(False)
            with eng.Else():
                run(True)

        block = ctx.enter_context(nc.Block())

        @block.sync
        def _(sp):
            sp.wait_ge(sem("pads_set"), 7)
            for tile, name in ((dst_i, "dst"), (src_i, "src"), (edge_w, "edge_weight"),
                               (t65_i, "edge_type_65"), (t8_i, "edge_type_8")):
                load_edges(sp, tile, A[name])
            x = A["x"]
            sp.dma_start(x_nm[SHIFT:BLK, 0, :], x[0:HEAD, :]).then_inc(sem("x_in"), 16)
            sp.dma_start(x_nm[:, 1:NB - 1, :],
                         x[HEAD:HEAD + (NB - 2) * BLK, :].rearrange("(b p) d -> p b d", p=BLK))\
              .then_inc(sem("x_in"), 16)
            sp.dma_start(x_nm[0:TAIL, NB - 1, :], x[N - TAIL:N, :]).then_inc(sem("x_in"), 16)
            for tile, w in small:
                sp.dma_start(tile[:, :], w).then_inc(sem("weights_in"), 16)
            for tile, w in cols:
                sp.dma_start(tile[:, :], w.rearrange("(d a) -> d a", a=1)).then_inc(sem("weights_in"), 16)
            sp.dma_start(gcn_b[:, :], A["L2_gnn_b"].rearrange("(a d) -> a d", a=1).to_broadcast([BLK, D]))\
              .then_inc(sem("weights_in"), 16)
            sp.dma_start(prelu_a[:, :], A["L2_gnn_prelu_a"].rearrange("(a d) -> a d", a=1)
                         .to_broadcast([BLK, 1])).then_inc(sem("weights_in"), 16)
            sp.dma_start(w8[:, :].rearrange("d (r k) -> d r k", k=D),
                         A["L3_gnn_W_rel"].rearrange("r d k -> d r k")).then_inc(sem("weights_in"), 16)
            w65_v = w65[:, :].rearrange("d (r k) -> d r k", k=D)
            sp.dma_start(w65_v, A["L1_gnn_W"][0].rearrange("r d k -> d r k")).then_inc(sem("w65_in", 0), 16)

            node_tables = {0: scratch["h1"], 1: scratch["h2"], 4: scratch["hw"]}
            wide_tables = {2: scratch["t65a"].rearrange("(n t) d -> n (t d)", t=R65),
                           3: scratch["t65b"].rearrange("(n t) d -> n (t d)", t=R65),
                           5: scratch["t8"].rearrange("(n t) d -> n (t d)", t=R8)}

            def rows(table, b):
                return table[b * BLK:(b + 1) * BLK, :] if isinstance(b, int) else \
                    table[bass.ds(b * BLK, BLK), :]

            def run(general):
                for p in range(PASSES):
                    if p == 3:
                        sp.wait_ge(sem("tab_act"), 5 * NB)
                        sp.wait_ge(sem("tab_dve"), 4 * NB)
                        sp.dma_start(w65_v, A["L1_gnn_W"][1].rearrange("r d k -> d r k"))\
                          .then_inc(sem("w65_in", 1), 16)

                    def finish(b, need):
                        if p in node_tables:
                            sp.wait_ge(sem("rows_ready"), before("rows_ready", p, general) + b + 1)
                            sp.dma_start(rows(node_tables[p], b), nm_blk[:, :]).then_inc(sem("stored"), 16)
                        elif p in (2, 3):
                            sp.wait_ge(sem("tab_act"), before("tab_act", p, general) + 5 * b + 5)
                            sp.wait_ge(sem("tab_dve"), before("tab_dve", p, general) + 4 * b + 4)
                            sp.dma_start(rows(wide_tables[p], b), table_blk[:, :])\
                              .then_inc(sem("stored"), 16)
                        elif p == 5:
                            sp.wait_ge(sem("rows_ready"), before("rows_ready", p, general) + b + 1)
                            sp.dma_start(rows(wide_tables[p], b), table_blk[:, 0:R8 * D])\
                              .then_inc(sem("stored"), 16)
                        else:
                            sp.wait_ge(sem("rows_ready"), before("rows_ready", p, general) + b + 1)
                            if isinstance(b, int) and b == 0:
                                sp.dma_start(out[0:HEAD, :], z_blk[SHIFT:BLK, :]).then_inc(sem("stored"), 16)
                            elif isinstance(b, int) and b == NB - 1:
                                sp.dma_start(out[N - TAIL:N, :], z_blk[0:TAIL, :]).then_inc(sem("stored"), 16)
                            else:
                                at0 = b * BLK - SHIFT
                                dst = out[at0:at0 + BLK, :] if isinstance(b, int) else \
                                    out[bass.ds(at0, BLK), :]
                                sp.dma_start(dst, z_blk[:, :]).then_inc(sem("stored"), 16)

                    finish(0, None)
                    with sp.Fori(1, NB - 1) as b:
                        finish(b, None)
                    finish(NB - 1, None)
                sp.wait_ge(sem("stored"), before("stored", PASSES, general))

            by_branch(sp, run)

        @block.gpsimd
        def _(pool):
            last = slice((NG - 1) * TILE, NG * TILE)
            pool.memset(src_i[:, last], 0).then_inc(sem("pads_set"), 1)
            pool.memset(dst_i[:, last], N - 1).then_inc(sem("pads_set"), 1)
            pool.memset(t65_i[:, last], 0).then_inc(sem("pads_set"), 1)
            pool.memset(t8_i[:, last], 0).then_inc(sem("pads_set"), 1)
            pool.memset(edge_w[:, last], 0.0).then_inc(sem("pads_set"), 1)
            pool.memset(x_nm[:, 0, :], 0.0).then_inc(sem("pads_set"), 1)
            pool.memset(x_nm[:, NB - 1, :], 0.0).then_inc(sem("pads_set"), 1)
            pool.iota(iota_win[:, :], pattern=[[1, WIN]], base=0, channel_multiplier=0,
                      allow_small_or_imprecise_dtypes=True).then_inc(sem("consts"), 1)
            pool.iota(iota_win_bf[:, :], pattern=[[1, WIN]], base=0, channel_multiplier=0,
                      allow_small_or_imprecise_dtypes=True).then_inc(sem("consts"), 1)
            pool.iota(iota_type[:, :], pattern=[[0, TILE], [1, R65]], base=0, channel_multiplier=0,
                      allow_small_or_imprecise_dtypes=True).then_inc(sem("consts"), 1)
            pool.iota(group_base[:, :], pattern=[[BLK, NG]], base=0, channel_multiplier=0,
                      allow_small_or_imprecise_dtypes=True).then_inc(sem("consts"), 1)
            pool.iota(sweep_base[:, :], pattern=[[WIN, SWEEPS]], base=0, channel_multiplier=0,
                      allow_small_or_imprecise_dtypes=True).then_inc(sem("consts"), 1)
            pool.memset(ident[:, :], 0.0).then_inc(sem("ident_zero"), 1)
            pool.memset(last_mask[:, :], 1.0).then_inc(sem("ident_zero"), 1)
            pool.memset(ones[:, :], 1.0).then_inc(sem("consts"), 1)
            pool.memset(zeros[:, :], 0.0).then_inc(sem("consts"), 1)
            pool.memset(eps[:, :], EPS).then_inc(sem("consts"), 1)
            pool.memset(mean_w[:, :], 0.0).then_inc(sem("consts"), 1)
            pool.memset(acc[:, :], 0.0).then_inc(sem("consts"), 1)
            pool.memset(counts[:, :], 0.0).then_inc(sem("consts"), 1)
            pool.wait_ge(sem("ident_zero"), 2)
            pool.affine_select(out=ident[:, :], in_=ident[:, :], compare_op=ALU.not_equal, fill=1.0,
                               base=0, pattern=[[-1, 128]], channel_multiplier=1).then_inc(sem("consts"), 1)
            pool.affine_select(out=last_mask[:, :], in_=last_mask[:, :], compare_op=ALU.is_ge, fill=0.0,
                               base=LAST - 1, pattern=[[-1, TILE]], channel_multiplier=-TILE)\
                .then_inc(sem("consts"), 1)

            def run(general):
                for p in range(PASSES):
                    table = gathers[p][0]
                    if p > 0:
                        pool.wait_ge(sem("stored"), before("stored", p, general))

                    def step(s, g, k, u, n):
                        if g is None:
                            return
                        pool.wait_ge(sem("rows_staged"), before("rows_staged", p, general) + s + 1)
                        pool.sem_inc(sem("gather_begun"), 1)
                        for j in range(TILE):
                            pool.indirect_dma_start(
                                out=msgs[:, u, j, :], out_offset=None, in_=table[:, :],
                                in_offset=bass.IndirectOffsetOnAxis(ap=rows_now[:, u, j:j + 1], axis=0))\
                                .then_inc(sem("gathered", p, u), 16)

                    schedule(pool, general, step, lambda b, need: None)
                pool.wait_ge(sem("stored"), before("stored", PASSES, general))

            by_branch(pool, run)

        @block.scalar
        def _(act):
            act.wait_ge(sem("consts"), 13)
            for n in range(-(-NB // 4)):
                w = min(4, NB - 4 * n) * BLK
                act.wait_ge(sem("x_turned"), n + 1)
                act.activation(x_fm[:, 4 * n * BLK:4 * n * BLK + w], tab_ps[n % 3][0:D, 0:w], ACT.Copy)\
                   .then_inc(sem("x_fm_done"), 1)
            act.wait_ge(sem("gcn_w_turned"), 1)
            act.activation(gcn_wt[:, :], post_ps[0:D, 0:D], ACT.Copy).then_inc(sem("gcn_wt_done"), 1)
            act.wait_ge(sem("edges_done"), 1)
            act.wait_ge(sem("weights_in"), WEIGHTS)

            def run(general):
                for p in range(PASSES):
                    def look_up(s, u):
                        for q in range(4):
                            act.wait_ge(sem("type_turned"), 4 * s + q + 1)
                            act.activation(type_hot_t[:, 4 * q:4 * q + 4, :]
                                           .rearrange("t j e -> t (j e)"),
                                           aux_ps[1][0:R65, :], ACT.Copy).then_inc(sem("type_hot_t_done"), 1)

                    def step(s, g, k, u, n):
                        if g is None:
                            return
                        act.wait_ge(sem("summed"), before("summed", p, general) + s + 1)
                        act.sem_inc(sem("act_turns"), 1)
                        act.activation(rows_now[:, u, :], col16(gathers[p][1], g), ACT.Copy)\
                           .then_inc(sem("rows_staged"), 1)

                    def extra(s, g, k, u):
                        if p == 1:
                            act.wait_ge(sem("look_done"), TILE // 2 * s + 1)
                            act.sem_inc(sem("act_turns"), 1)
                            base = (k * WIN if general else g * BLK)
                            act.activation(inv_now[:, :], at(counts, base, WIN), ACT.Copy)\
                               .then_inc(sem("inv_staged"), 1)
                            look_up(s, u)

                    def norm(b):
                        act.wait_ge(sem("moments"), before("moments", p, general) + b + 1)
                        act.activation(std[:, :], mean_var[:, 1:2], ACT.Sqrt, bias=eps[0:BLK, :])\
                           .then_inc(sem("std_done"), 1)

                    def back(b):
                        act.wait_ge(sem("z_turned"), before("z_turned", p, general) + b + 1)
                        act.sem_inc(sem("act_turns"), 1)
                        act.activation(cols_of(x_fm, b), fm_a[0:D, :], ACT.Copy)
                        act.activation(xblk[:, :], fm_a[0:D, :], ACT.Copy).then_inc(sem("xblk_done"), 1)

                    def table(b):
                        for c in range(0, len(CHUNKS), 2):
                            o, w = CHUNKS[c]
                            if c == 0 and not (isinstance(b, int) and b == 0):
                                act.wait_ge(sem("stored"), before("stored", p, general) + 16 * b)
                            act.wait_ge(sem("tab_mult"), before("tab_mult", p, general) + 9 * b + c + 1)
                            act.activation(table_blk[:, o:o + w], tab_ps[c % 3][0:BLK, 0:w], ACT.Copy)\
                               .then_inc(sem("tab_act"), 1)

                    def finish(b, need):
                        if p in GIN:
                            f = gin_w1[p].shape[1]
                            act.wait_ge(sem("hidden"), before("hidden", p, general) + b + 1)
                            act.activation(hid_blk[0:f, :], fm_a[0:f, :], ACT.Relu, bias=gin_b1[p][:, :])\
                               .then_inc(sem("hidden_relu"), 1)
                            act.wait_ge(sem("gin_out"), before("gin_out", p, general) + b + 1)
                            act.sem_inc(sem("act_turns"), 1)
                            if p < 2:
                                act.activation(cols_of(h_fm, b), fm_b[0:D, :], ACT.Relu, bias=gin_b2[p][:, :])
                                act.activation(out_blk[:, :], fm_b[0:D, :], ACT.Relu, bias=gin_b2[p][:, :])\
                                   .then_inc(sem("out_done"), 1)
                            else:
                                act.activation(out_blk[:, :], fm_b[0:D, :], ACT.Identity,
                                               bias=gin_b2[p][:, :]).then_inc(sem("out_done"), 1)
                                norm(b)
                                back(b)
                                table(b)
                        elif p in RGCN:
                            act.wait_ge(sem("conv_sum"), before("conv_sum", p, general) + b + 1)
                            act.activation(out_blk[:, :], y_blk[:, :], ACT.Relu, bias=rg_b[p - 3][:, :])
                            act.activation(res_blk[:, :], fm_b[0:D, :], ACT.Relu, bias=res_b[p - 3][:, :])\
                               .then_inc(sem("conv_relu"), 1)
                            if p == 3:
                                table(b)
                            else:
                                norm(b)
                                back(b)
                        elif p == GCN:
                            norm(b)
                            back(b)
                            act.wait_ge(sem("encoded"), before("encoded", p, general) + b + 1)
                            act.sem_inc(sem("act_turns"), 1)
                            act.activation(cols_of(h_fm, b), fm_b[0:D, :], ACT.Relu, bias=b_enc[:, :])
                            act.activation(out_blk[:, :], fm_b[0:D, :], ACT.Relu, bias=b_enc[:, :])\
                               .then_inc(sem("out_done"), 1)
                            if not (isinstance(b, int) and b == 0):
                                act.wait_ge(sem("stored"), before("stored", p, general) + 16 * b)
                            act.wait_ge(sem("tab_mult"), before("tab_mult", p, general) + b + 1)
                            act.activation(table_blk[:, 0:R8 * D], tab_ps[0][0:BLK, 0:R8 * D], ACT.Copy)\
                               .then_inc(sem("rows_ready"), 1)
                        else:
                            act.wait_ge(sem("conv_sum"), before("conv_sum", p, general) + b + 1)
                            act.activation(out_blk[:, :], y_blk[:, :], ACT.Relu, bias=rel_b[:, :])\
                               .then_inc(sem("conv_relu"), 1)
                            norm(b)

                    if p == 1:
                        act.wait_ge(sem("inverse_done"), 1)
                    schedule(act, general, step, finish, extra)
                    if p == 0:
                        act.wait_ge(sem("degrees"), 1)
                        act.activation(dinv[:, :], aux_ps[0][0:BLK, 0:NB], ACT.Sqrt, bias=ones[0:BLK, :])\
                           .then_inc(sem("degree_root"), 1)

            by_branch(act, run)

        @block.tensor
        def _(pe):
            pe.wait_ge(sem("consts"), 13)
            pe.wait_ge(sem("x_in"), 48)
            for n in range(-(-NB // 4)):
                if n >= 3:
                    pe.wait_ge(sem("x_fm_done"), n - 2)
                for b in range(4 * n, min(4 * n + 4, NB)):
                    o = (b % 4) * BLK
                    last = pe.transpose(tab_ps[n % 3][0:D, o:o + BLK], x_nm[:, b, :], ident[0:BLK, 0:BLK])
                last.then_inc(sem("x_turned"), 1)
            pe.wait_ge(sem("weights_in"), WEIGHTS)
            pe.transpose(post_ps[0:D, 0:D], gcn_w[:, :], ident[0:D, 0:D]).then_inc(sem("gcn_w_turned"), 1)
            pe.wait_ge(sem("gcn_wt_done"), 1)
            pe.wait_ge(sem("outside_done"), 1)
            pe.matmul(post_ps[0:1, 0:1], flag_f[:, :], ones[:, :]).then_inc(sem("outside_sum"), 1)
            pe.sem_inc(sem("summed"), 2)
            pe.sem_inc(sem("look_done"), 1)

            def run(general):
                for p in range(PASSES):
                    def look_up(s):
                        pe.wait_ge(sem("type_hot_done"), s + 1)
                        for q in range(4):
                            pe.wait_ge(sem("type_hot_t_done"), 4 * s + q + 1)
                            for j in range(4 * q, 4 * q + 4):
                                last = pe.transpose(aux_ps[1][0:R65, (j % 4) * 128:(j % 4 + 1) * 128],
                                                    type_hot[:, j, :], ident[:, :])
                            last.then_inc(sem("type_turned"), 1)
                        pe.wait_ge(sem("inv_staged"), s + 1)
                        pe.wait_ge(sem("type_hot_t_done"), 4 * s + 5)
                        for j in range(TILE):
                            if j % 2 == 0:
                                pe.wait_ge(sem("look_used"), TILE // 2 * s + j // 2 + 1)
                            last = pe.matmul(tab_ps[j // 2 % 2][:, (j % 2) * WIN:(j % 2 + 1) * WIN],
                                             type_hot_t[:, j, :], inv_now[:, :])
                            if j % 2:
                                last.then_inc(sem("look_done"), 1)

                    def step(s, g, k, u, n):
                        if g is None:
                            return
                        if p == 0:
                            pe.wait_ge(sem("type_hot_bf_done"), s + 2)
                            for j in range(TILE):
                                pe.matmul(aux_ps[u][0:R65, 0:WIN], type_hot_bf[:, j, :], hot_bf[:, j, :],
                                          start=(j == 0), stop=(j == TILE - 1))
                        if p == 1:
                            look_up(s)
                        pe.wait_ge(sem("hot_done"), before("hot_done", p, general) + s + 2)
                        pe.wait_ge(sem("gathered", p, u), 16 * TILE * (n + 1))
                        for j in range(TILE):
                            last = pe.matmul(sum_ps[u][0:D, 0:WIN], msgs[:, u, j, :], hot[:, u, j, :],
                                             start=(j == 0), stop=(j == TILE - 1))
                        last.then_inc(sem("summed"), 1)

                    def norm(b, fm):
                        if p != GCN:
                            pe.wait_ge(sem("y_done"), before("y_done", p, general) + b + 1)
                            pe.sem_inc(sem("pe_turns"), 1)
                            pe.transpose(nm_ps, y_blk[:, :], ident[0:D, 0:D]).then_inc(sem("y_turned"), 1)
                        if fm:
                            pe.wait_ge(sem("z_done"), before("z_done", p, general) + b + 1)
                            pe.sem_inc(sem("pe_turns"), 1)
                            pe.transpose(fm_a[0:D, :], z_blk[:, :], ident[0:BLK, 0:BLK])\
                              .then_inc(sem("z_turned"), 1)

                    def table(b):
                        if isinstance(b, int) and b == 0:
                            pe.wait_ge(sem("w65_in", p - 2), 16)
                        pe.wait_ge(sem("xblk_done"), before("xblk_done", p, general) + b + 1)
                        pe.sem_inc(sem("pe_turns"), 1)
                        for c, (o, w) in enumerate(CHUNKS):
                            if c >= 3:
                                if c % 2:
                                    pe.wait_ge(sem("tab_act"), before("tab_act", p, general) + 5 * b + (c - 3) // 2 + 1)
                                else:
                                    pe.wait_ge(sem("tab_dve"), before("tab_dve", p, general) + 4 * b + (c - 3) // 2 + 1)
                            pe.matmul(tab_ps[c % 3][0:BLK, 0:w], xblk[:, :], w65[:, o:o + w])\
                              .then_inc(sem("tab_mult"), 1)

                    def finish(b, need):
                        if p in GIN:
                            f = gin_w1[p].shape[1]
                            pe.wait_ge(sem("in_done"), before("in_done", p, general) + b + 1)
                            pe.sem_inc(sem("pe_turns"), 1)
                            pe.matmul(fm_a[0:f, :], gin_w1[p][:, :], in_blk[:, :]).then_inc(sem("hidden"), 1)
                            pe.wait_ge(sem("hidden_relu"), before("hidden_relu", p, general) + b + 1)
                            pe.sem_inc(sem("pe_turns"), 1)
                            pe.matmul(fm_b[0:D, :], gin_w2[p][:, :], hid_blk[0:f, :])\
                              .then_inc(sem("gin_out"), 1)
                            if p < 2:
                                pe.wait_ge(sem("out_done"), before("out_done", p, general) + b + 1)
                                pe.sem_inc(sem("pe_turns"), 1)
                                pe.transpose(nm_ps, out_blk[:, :], ident[0:D, 0:D])\
                                  .then_inc(sem("out_turned"), 1)
                            else:
                                norm(b, True)
                                table(b)
                        elif p in RGCN:
                            pe.wait_ge(sem("in_done"), before("in_done", p, general) + b + 1)
                            pe.sem_inc(sem("pe_turns"), 1)
                            pe.matmul(fm_a[0:D, :], root[p - 3][:, :], in_blk[:, :])
                            pe.matmul(fm_b[0:D, :], res_w[p - 3][:, :], in_blk[:, :])\
                              .then_inc(sem("conv_mult"), 1)
                            if p == 3:
                                table(b)
                            else:
                                norm(b, True)
                                pe.wait_ge(sem("xblk_done"), before("xblk_done", p, general) + b + 1)
                                pe.sem_inc(sem("pe_turns"), 1)
                                pe.matmul(nm_ps, xblk[:, :], gcn_wt[:, :]).then_inc(sem("gcn_mult"), 1)
                        elif p == GCN:
                            pe.wait_ge(sem("in_done"), before("in_done", p, general) + b + 1)
                            pe.sem_inc(sem("pe_turns"), 1)
                            pe.transpose(nm_ps, in_blk[:, :], ident[0:D, 0:D]).then_inc(sem("sum_turned"), 1)
                            norm(b, True)
                            pe.wait_ge(sem("xblk_done"), before("xblk_done", p, general) + b + 1)
                            pe.sem_inc(sem("pe_turns"), 1)
                            pe.matmul(fm_b[0:D, :], w_enc[:, :], xblk[:, :]).then_inc(sem("encoded"), 1)
                            pe.wait_ge(sem("out_done"), before("out_done", p, general) + b + 1)
                            pe.sem_inc(sem("pe_turns"), 1)
                            pe.matmul(tab_ps[0][0:BLK, 0:R8 * D], out_blk[:, :], w8[:, :])\
                              .then_inc(sem("tab_mult"), 1)
                        else:
                            pe.wait_ge(sem("in_done"), before("in_done", p, general) + b + 1)
                            pe.sem_inc(sem("pe_turns"), 1)
                            pe.matmul(fm_a[0:D, :], w_self[:, :], in_blk[:, :]).then_inc(sem("conv_mult"), 1)
                            norm(b, False)

                    schedule(pe, general, step, finish, finish_first=True)
                    if p == 0:
                        pe.wait_ge(sem("counts_done"), SWEEPS * NG if general else NG)
                        for b in range(NB):
                            last = pe.matmul(aux_ps[0][0:BLK, b:b + 1], counts[:, b * BLK:(b + 1) * BLK],
                                             ones[0:R65, :])
                        last.then_inc(sem("degrees"), 1)

            by_branch(pe, run)

        @block.vector
        def _(dve):
            dve.wait_ge(sem("consts"), 13)
            dve.wait_ge(sem("edges_in"), 15 * 16)
            dve.tensor_scalar(slot_f[:, :], dst_i[:, :], float(SHIFT), None, ALU.add).then_inc(sem("prep"), 1)
            dve.tensor_scalar(row_slot[:, :], src_i[:, :], SHIFT, None, ALU.add).then_inc(sem("prep"), 1)
            dve.tensor_copy(t65_f[:, :], t65_i[:, :]).then_inc(sem("prep"), 1)
            dve.wait_ge(sem("prep"), 3)
            dve.tensor_tensor(scratch_f[:, :].rearrange("p (g j) -> p g j", j=TILE),
                              slot_f[:, :].rearrange("p (g j) -> p g j", j=TILE),
                              group_base[:, :].unsqueeze(2).to_broadcast([128, NG, TILE]), ALU.subtract)\
               .then_inc(sem("prep"), 1)
            dve.scalar_tensor_tensor(out=row_65[:, :], in0=row_slot[:, :], scalar=float(R65),
                                     in1=t65_i[:, :], op0=ALU.mult, op1=ALU.add).then_inc(sem("prep"), 1)
            dve.scalar_tensor_tensor(out=row_8[:, :], in0=row_slot[:, :], scalar=float(R8),
                                     in1=t8_i[:, :], op0=ALU.mult, op1=ALU.add).then_inc(sem("prep"), 1)
            dve.wait_ge(sem("prep"), 6)
            dve.tensor_reduce(worst[:, 0:1], scratch_f[:, :], AX.X, ALU.max).then_inc(sem("prep"), 1)
            dve.tensor_reduce(worst[:, 1:2], scratch_f[:, :], AX.X, ALU.min).then_inc(sem("prep"), 1)
            dve.wait_ge(sem("prep"), 8)
            dve.tensor_scalar(worst[:, 0:1], worst[:, 0:1], float(WIN - 1), None, ALU.is_gt)\
               .then_inc(sem("prep"), 1)
            dve.tensor_scalar(worst[:, 1:2], worst[:, 1:2], 0.0, None, ALU.is_lt).then_inc(sem("prep"), 1)
            dve.wait_ge(sem("prep"), 10)
            dve.tensor_tensor(flag_f[:, :], worst[:, 0:1], worst[:, 1:2], ALU.add)\
               .then_inc(sem("outside_done"), 1)
            lastg = slot_f[:, (NG - 1) * TILE:NG * TILE]
            dve.scalar_tensor_tensor(out=lastg, in0=lastg, scalar=NOWHERE, in1=last_mask[:, :],
                                     op0=ALU.add, op1=ALU.mult).then_inc(sem("prep"), 1)
            dve.wait_ge(sem("prep"), 11)
            dve.tensor_scalar(lastg, lastg, -NOWHERE, None, ALU.add).then_inc(sem("edges_done"), 1)
            dve.wait_ge(sem("outside_sum"), 1)
            dve.tensor_scalar(flag_i[:, :], post_ps[0:1, 0:1], 0.5, None, ALU.is_gt)\
               .then_inc(sem("flag_ready"), 1)
            dve.wait_ge(sem("edges_done"), 1)
            dve.wait_ge(sem("x_fm_done"), -(-NB // 4))
            dve.wait_ge(sem("weights_in"), WEIGHTS)
            dve.sem_inc(sem("hot_done"), 1)
            dve.sem_inc(sem("type_hot_bf_done"), 1)
            dve.sem_inc(sem("look_used"), 2)
            dve.sem_inc(sem("type_hot_t_done"), 1)

            def run(general):
                for p in range(PASSES):
                    scale = edge_scale[p]

                    def step(s, g, k, u, n):
                        first = isinstance(s, int) and s == 0
                        if g is not None:
                            dve.wait_ge(sem("summed"), before("summed", p, general) + s + 1)
                            dve.wait_ge(sem("hot_done"), before("hot_done", p, general) + s + 1)
                            if p == 0:
                                dve.wait_ge(sem("type_hot_bf_done"), s + 1)
                            base = at(sweep_base, k) if general else at(group_base, g)
                            dve.tensor_scalar(rel_now[:, :], col16(slot_f, g), base, None, ALU.subtract)\
                               .then_inc(sem("staged"), 1)
                            if scale is not None:
                                dve.tensor_copy(w_now[:, :], col16(scale, g)).then_inc(sem("staged"), 1)
                            dve.wait_ge(sem("staged"), before("staged", p, general) + (s + 1) * (2 if scale is not None else 1))
                            for j in range(TILE):
                                if scale is None:
                                    last = dve.tensor_scalar(hot[:, u, j, :], iota_win[:, :],
                                                             rel_now[:, j:j + 1], None, ALU.is_equal)
                                else:
                                    last = dve.tensor_scalar(hot[:, u, j, :], iota_win[:, :],
                                                             rel_now[:, j:j + 1], w_now[:, j:j + 1],
                                                             ALU.is_equal, ALU.mult)
                            last.then_inc(sem("hot_done"), 1)
                        if not general and not first:
                            add_sums(s - 1, (s - 1) * BLK, 1 - u if u is not None else (NG - 1) % 2)

                    def add_sums(s, base, u):
                        dve.wait_ge(sem("summed"), before("summed", p, general) + s + 3)
                        dve.tensor_tensor(at(acc, base, WIN), at(acc, base, WIN), sum_ps[u][0:D, 0:WIN],
                                          ALU.add).then_inc(sem("added"), 1)
                        if p == 0:
                            dve.tensor_tensor(at(counts, base, WIN), at(counts, base, WIN),
                                              aux_ps[u][0:R65, 0:WIN], ALU.add)\
                               .then_inc(sem("counts_done"), 1)
                            dve.wait_ge(sem("counts_done"), s + 1)
                        dve.wait_ge(sem("added"), before("added", p, general) + s + 1)
                        dve.sem_inc(sem("dve_turns"), 1)

                    def type_one_hot(tile, g):
                        return dve.tensor_tensor(
                            tile[:, :, :], iota_type[:, :].rearrange("p (j t) -> p j t", t=R65),
                            col16(t65_f, g).unsqueeze(2).to_broadcast([128, TILE, R65]), ALU.is_equal)

                    def extra(s, g, k, u):
                        if p == 0:
                            dve.wait_ge(sem("summed"), before("summed", p, general) + s + 2)
                            for j in range(TILE):
                                dve.tensor_scalar(hot_bf[:, j, :], iota_win_bf[:, :], rel_now[:, j:j + 1],
                                                  None, ALU.is_equal)
                            type_one_hot(type_hot_bf, g).then_inc(sem("type_hot_bf_done"), 1)
                        if p == 1:
                            type_one_hot(type_hot, g).then_inc(sem("type_hot_done"), 1)
                            for j in range(TILE):
                                if j % 2 == 0:
                                    dve.wait_ge(sem("look_done"), TILE // 2 * s + j // 2 + 2)
                                last = dve.scalar_tensor_tensor(
                                    out=junk[:, j % 4, :], in0=iota_win[:, :], scalar=rel_now[:, j:j + 1],
                                    in1=tab_ps[j // 2 % 2][:, (j % 2) * WIN:(j % 2 + 1) * WIN],
                                    op0=ALU.is_equal, op1=ALU.mult, accum_out=mean_now[:, j:j + 1])
                                if j % 2:
                                    last.then_inc(sem("look_used"), 1)
                            dve.wait_ge(sem("look_used"), TILE // 2 * s + TILE // 2 + 2)
                            dve.tensor_tensor(col16(mean_w, g), col16(mean_w, g), mean_now[:, :], ALU.add)\
                               .then_inc(sem("mean_w_done"), 1)
                            dve.wait_ge(sem("mean_w_done"), s + 1)
                        if general:
                            add_sums(s, k * WIN, u)

                    def clear(b):
                        dve.tensor_copy(cols_of(acc, b), zeros[:, :]).then_inc(sem("cleared"), 1)

                    def norm(b, y):
                        dve.bn_stats(stats[:, :], y).then_inc(sem("stats"), 1)
                        dve.wait_ge(sem("stats"), before("stats", p, general) + b + 1)
                        dve.sem_inc(sem("dve_turns"), 1)
                        dve.bn_aggr(mean_var[:, :], stats[:, :]).then_inc(sem("moments"), 1)
                        dve.wait_ge(sem("std_done"), before("std_done", p, general) + b + 1)
                        dve.reciprocal(rstd[:, :], std[:, :]).then_inc(sem("rstd"), 1)
                        dve.wait_ge(sem("rstd"), before("rstd", p, general) + b + 1)
                        if p == 4:
                            dve.tensor_scalar(nm_at(x_nm, b), y, mean_var[:, 0:1], rstd[:, :],
                                              ALU.subtract, ALU.mult)
                        if p == REL and not (isinstance(b, int) and b == 0):
                            dve.wait_ge(sem("stored"), before("stored", p, general) + 16 * b)
                        dve.tensor_scalar(z_blk[:, :], y, mean_var[:, 0:1], rstd[:, :],
                                          ALU.subtract, ALU.mult)\
                           .then_inc(sem("rows_ready" if p == REL else "z_done"), 1)

                    def finish(b, need):
                        if p in GIN:
                            dve.tensor_tensor(in_blk[:, :], cols_of(acc, b),
                                              cols_of(x_fm if p == 0 else h_fm, b), ALU.add)\
                               .then_inc(sem("in_done"), 1)
                            if p < 2:
                                dve.wait_ge(sem("out_turned"), before("out_turned", p, general) + b + 1)
                                if not (isinstance(b, int) and b == 0):
                                    dve.wait_ge(sem("stored"), before("stored", p, general) + 16 * b)
                                dve.tensor_copy(nm_blk[:, :], nm_ps).then_inc(sem("rows_ready"), 1)
                                clear(b)
                                return
                            dve.wait_ge(sem("out_done"), before("out_done", p, general) + b + 1)
                            dve.tensor_tensor(y_blk[:, :], out_blk[:, :], cols_of(x_fm, b), ALU.add)\
                               .then_inc(sem("y_done"), 1)
                            clear(b)
                            dve.wait_ge(sem("y_turned"), before("y_turned", p, general) + b + 1)
                            norm(b, nm_ps)
                            table(b)
                        elif p in RGCN:
                            dve.tensor_copy(in_blk[:, :], cols_of(x_fm if p == 3 else h_fm, b))\
                               .then_inc(sem("in_done"), 1)
                            dve.wait_ge(sem("conv_mult"), before("conv_mult", p, general) + b + 1)
                            dve.tensor_tensor(y_blk[:, :], fm_a[0:D, :], cols_of(acc, b), ALU.add)\
                               .then_inc(sem("conv_sum"), 1)
                            dve.wait_ge(sem("conv_relu"), before("conv_relu", p, general) + b + 1)
                            if p == 3:
                                dve.tensor_tensor(cols_of(h_fm, b), out_blk[:, :], res_blk[:, :], ALU.add)
                                dve.tensor_tensor(xblk[:, :], out_blk[:, :], res_blk[:, :], ALU.add)\
                                   .then_inc(sem("xblk_done"), 1)
                                clear(b)
                                table(b)
                                return
                            dve.tensor_tensor(res_blk[:, :], out_blk[:, :], res_blk[:, :], ALU.add)\
                               .then_inc(sem("h2_done"), 1)
                            clear(b)
                            dve.wait_ge(sem("h2_done"), b + 1)
                            dve.tensor_tensor(y_blk[:, :], res_blk[:, :], cols_of(x_fm, b), ALU.add)\
                               .then_inc(sem("y_done"), 1)
                            dve.wait_ge(sem("y_turned"), before("y_turned", p, general) + b + 1)
                            norm(b, nm_ps)
                            dve.wait_ge(sem("gcn_mult"), before("gcn_mult", p, general) + b + 1)
                            dve.tensor_scalar(nm_at(hws_nm, b), nm_ps, at(dinv, b), None, ALU.mult)
                            if not (isinstance(b, int) and b == 0):
                                dve.wait_ge(sem("stored"), before("stored", p, general) + 16 * b)
                            dve.tensor_scalar(nm_blk[:, :], nm_ps, at(dinv, b), None, ALU.mult)\
                               .then_inc(sem("rows_ready"), 1)
                        elif p == GCN:
                            dve.tensor_copy(in_blk[:, :], cols_of(acc, b)).then_inc(sem("in_done"), 1)
                            dve.wait_ge(sem("sum_turned"), before("sum_turned", p, general) + b + 1)
                            dve.tensor_tensor(y_nm[:, :], nm_ps, nm_at(hws_nm, b), ALU.add)\
                               .then_inc(sem("gcn_steps"), 1)
                            clear(b)
                            dve.wait_ge(sem("gcn_steps"), 4 * b + 1)
                            dve.scalar_tensor_tensor(out=y_nm[:, :], in0=y_nm[:, :], scalar=at(dinv, b),
                                                     in1=gcn_b[:, :], op0=ALU.mult, op1=ALU.add)\
                               .then_inc(sem("gcn_steps"), 1)
                            dve.wait_ge(sem("gcn_steps"), 4 * b + 2)
                            dve.tensor_scalar(neg_nm[:, :], y_nm[:, :], 0.0, prelu_a[:, :], ALU.min, ALU.mult)\
                               .then_inc(sem("gcn_steps"), 1)
                            dve.wait_ge(sem("gcn_steps"), 4 * b + 3)
                            dve.scalar_tensor_tensor(out=y_nm[:, :], in0=y_nm[:, :], scalar=0.0,
                                                     in1=neg_nm[:, :], op0=ALU.max, op1=ALU.add)\
                               .then_inc(sem("gcn_steps"), 1)
                            dve.wait_ge(sem("gcn_steps"), 4 * b + 4)
                            dve.tensor_tensor(y_nm[:, :], y_nm[:, :], nm_at(x_nm, b), ALU.add)\
                               .then_inc(sem("y_done"), 1)
                            dve.wait_ge(sem("y_done"), before("y_done", p, general) + b + 1)
                            norm(b, y_nm[:, :])
                        else:
                            dve.tensor_copy(in_blk[:, :], cols_of(h_fm, b)).then_inc(sem("in_done"), 1)
                            dve.wait_ge(sem("conv_mult"), before("conv_mult", p, general) + b + 1)
                            dve.tensor_tensor(y_blk[:, :], fm_a[0:D, :], cols_of(acc, b), ALU.add)\
                               .then_inc(sem("conv_sum"), 1)
                            dve.wait_ge(sem("conv_relu"), before("conv_relu", p, general) + b + 1)
                            dve.tensor_tensor(res_blk[:, :], out_blk[:, :], cols_of(h_fm, b), ALU.add)\
                               .then_inc(sem("h_sum"), 1)
                            dve.wait_ge(sem("h_sum"), b + 1)
                            dve.tensor_tensor(y_blk[:, :], res_blk[:, :], cols_of(x_fm, b), ALU.add)\
                               .then_inc(sem("y_done"), 1)
                            dve.wait_ge(sem("y_turned"), before("y_turned", p, general) + b + 1)
                            norm(b, nm_ps)

                    def table(b):
                        for c in range(1, len(CHUNKS), 2):
                            o, w = CHUNKS[c]
                            if c == 1 and not (isinstance(b, int) and b == 0):
                                dve.wait_ge(sem("stored"), before("stored", p, general) + 16 * b)
                            dve.wait_ge(sem("tab_mult"), before("tab_mult", p, general) + 9 * b + c + 1)
                            dve.tensor_copy(table_blk[:, o:o + w], tab_ps[c % 3][0:BLK, 0:w])\
                               .then_inc(sem("tab_dve"), 1)

                    if p > 0:
                        dve.wait_ge(sem("cleared"), before("cleared", p, general))
                    schedule(dve, general, step, finish, extra)
                    if p == 0:
                        dve.wait_ge(sem("degree_root"), 1)
                        dve.reciprocal(dinv[:, :], dinv[:, :]).then_inc(sem("dinv_done"), 1)
                        dve.tensor_scalar(counts[:, :], counts[:, :], 1.0, None, ALU.max)\
                           .then_inc(sem("counts_max"), 1)
                        dve.wait_ge(sem("counts_max"), 1)
                        dve.reciprocal(counts[:, :], counts[:, :]).then_inc(sem("inverse_done"), 1)

            by_branch(dve, run)


_INS = ["x", "src", "dst", "edge_type_65", "edge_type_8", "edge_weight",
        "L0_gnn_w11", "L0_gnn_b11", "L0_gnn_w12", "L0_gnn_b12", "L0_gnn_w21", "L0_gnn_b21",
        "L0_gnn_w22", "L0_gnn_b22", "L0_gnn_w31", "L0_gnn_b31", "L0_gnn_w32", "L0_gnn_b32",
        "L1_gnn_W", "L1_gnn_root", "L1_gnn_bias", "L1_gnn_res_W", "L1_gnn_res_b",
        "L2_gnn_W", "L2_gnn_b", "L2_gnn_prelu_a",
        "L3_gnn_W_enc", "L3_gnn_b_enc", "L3_gnn_W_rel", "L3_gnn_W_self", "L3_gnn_bias"]


def kernel(**inputs):
    import numpy as _np
    import concourse.bacc as _bacc
    from concourse import mybir as _mybir
    from concourse.bass_utils import run_bass_kernel_spmd as _run

    nc = _bacc.Bacc("TRN2", target_bir_lowering=False, num_devices=1)
    arrays, args = {}, {}
    for name in _INS:
        a = _np.ascontiguousarray(inputs[name])
        arrays[f"in_{name}_dram"] = a
        args[name] = nc.dram_tensor(f"in_{name}_dram", a.shape, _mybir.dt.from_np(a.dtype),
                                    kind="ExternalInput").ap()
    n, d = inputs["x"].shape
    rows = -(-(n + SHIFT) // BLK) * BLK
    sizes = {"h1": rows, "h2": rows, "hw": rows, "t8": rows * 8, "t65a": rows * 65, "t65b": rows * 65}
    scratch = {name: nc.dram_tensor(f"table_{name}", (r, d), F32, kind="Internal").ap()
               for name, r in sizes.items()}
    out = nc.dram_tensor("out_0_dram", (n, d), _mybir.dt.float32, kind="ExternalOutput").ap()
    bass_gnn(nc, args, out, scratch)
    r = _run(nc, [arrays], core_ids=[0])
    return r.results[0]["out_0_dram"]
```

```python
from contextlib import ExitStack

import concourse.bass as bass
from concourse import mybir

F32 = mybir.dt.float32
BF16 = mybir.dt.bfloat16
I32 = mybir.dt.int32
ALU = mybir.AluOpType
ACT = mybir.ActivationFunctionType
AX = mybir.AxisListType

D = 64
TILE = 16
QUART = TILE // 4
GROUP = 128 * TILE
WIN = 200
STEP = 119
SHIFT = 20
BLK = 125
NOWHERE = 10000.0
EPS = 1e-5
PASSES = 7
GIN, RGCN, GCN, REL = (0, 1, 2), (3, 4), 5, 6


def bass_gnn(nc, A, out, scratch):
    N = A["x"].shape[0]
    E = A["src"].shape[0]
    R65 = A["L1_gnn_W"].shape[1]
    R8 = A["L3_gnn_W_rel"].shape[0]
    NG = -(-E // GROUP)
    NB = N // BLK
    SLOTS = -(-(N + SHIFT) // WIN) * WIN
    SWEEPS = SLOTS // WIN
    LAST = E - (NG - 1) * GROUP
    TW = R65 * D
    CHUNKS = [(c, min(512, TW - c)) for c in range(0, TW, 512)]
    PHASES = 5
    XBANKS = -(-NB // 4)
    assert NG % 2 == 0 and NB == NG - 1 and NB * BLK == N and STEP * (NG - 1) + WIN <= SLOTS
    PAIRS = NG // 2

    with ExitStack() as ctx:
        def sb(name, shape, dt=F32):
            return ctx.enter_context(nc.sbuf_tensor(name, shape, dt))

        def pb(name):
            return ctx.enter_context(nc.psum_tensor(name, [128, 512], F32))

        sems = {}

        def sem(*name):
            key = "_".join(str(x) for x in name)
            if key not in sems:
                sems[key] = ctx.enter_context(nc.semaphore("s_" + key))
            return sems[key]

        src_i = sb("src_i", [128, NG * TILE], I32)
        dst_i = sb("dst_i", [128, NG * TILE], I32)
        t65_i = sb("t65_i", [128, NG * TILE], I32)
        t8_i = sb("t8_i", [128, NG * TILE], I32)
        edge_w = sb("edge_w", [128, NG * TILE])
        row_65 = sb("row_65", [128, NG * TILE], I32)
        row_8 = sb("row_8", [128, NG * TILE], I32)
        slot_f = sb("slot_f", [128, NG * TILE])
        t65_f = sb("t65_f", [128, NG * TILE])
        mean_w = sb("mean_w", [128, NG * TILE])
        above_window = sb("above_window", [128, NG * TILE])
        above_block = sb("above_block", [128, NG * TILE])
        last_mask = sb("last_mask", [128, TILE])
        iota_win = sb("iota_win", [128, WIN])
        iota_win_bf = sb("iota_win_bf", [128, WIN], BF16)
        iota_type = sb("iota_type", [128, TILE * R65], BF16)
        group_base = sb("group_base", [128, NG])
        block_base = sb("block_base", [128, NG])
        sweep_base = sb("sweep_base", [128, SWEEPS])
        ident = sb("ident", [128, 128])
        ident_bf = sb("ident_bf", [128, 128], BF16)
        ident_twice = sb("ident_twice", [D, 2, D])
        ones = sb("ones", [128, 1])
        zeros = sb("zeros", [D, BLK])
        eps = sb("eps", [128, 1])
        worst = sb("worst", [128, 3])
        flag_f = sb("flag_f", [128, 1])
        flag_i = sb("flag_i", [1, 1], I32)
        rows_now = sb("rows_now", [128, 2, TILE], I32)
        msgs = sb("msgs", [128, 2, TILE, D])
        hot = sb("hot", [128, 2, TILE, WIN])
        rel_now = sb("rel_now", [128, 2, TILE])
        w_now = sb("w_now", [128, 2, TILE])
        hot_bf = sb("hot_bf", [128, TILE, WIN], BF16)
        type_hot = sb("type_hot", [128, TILE, R65], BF16)
        type_hot_t = sb("type_hot_t", [R65, TILE, 128], BF16)
        inv_now = sb("inv_now", [R65, 3, WIN], BF16)
        inv_rest = sb("inv_rest", [R65, WIN])
        mean_now = sb("mean_now", [128, TILE])
        junk = sb("junk", [128, 4, WIN])
        acc = sb("acc", [D, SLOTS])
        counts = sb("counts", [R65, SLOTS])
        x_fm = sb("x_fm", [D, N])
        h_fm = sb("h_fm", [D, N])
        x_nm = sb("x_nm", [BLK, NB, D])
        hws_nm = sb("hws_nm", [BLK, NB, D])
        dinv = sb("dinv", [BLK, NB])
        in_blk = sb("in_blk", [D, BLK])
        hid_blk = sb("hid_blk", [128, BLK])
        out_blk = sb("out_blk", [D, BLK])
        res_blk = sb("res_blk", [D, BLK])
        y_blk = sb("y_blk", [D, BLK])
        xblk = sb("xblk", [D, BLK])
        x_hi_mid = sb("x_hi_mid", [128, BLK], BF16)
        x_hi_lo = sb("x_hi_lo", [128, BLK], BF16)
        x_rest = sb("x_rest", [128, BLK])
        nm_blk = sb("nm_blk", [BLK, D])
        z_blk = sb("z_blk", [BLK, 2, D])
        y_nm = sb("y_nm", [BLK, D])
        neg_nm = sb("neg_nm", [BLK, D])
        stats = sb("stats", [BLK, 6])
        mean_var = sb("mean_var", [BLK, 2])
        std = sb("std", [BLK, 1])
        rstd = sb("rstd", [BLK, 1])
        table_blk = sb("table_blk", [128, TW])
        w_hi = sb("w_hi", [128, TW], BF16)
        w_mid = sb("w_mid", [128, TW], BF16)
        w_lo_hi = sb("w_lo_hi", [128, TW], BF16)
        w8 = sb("w8", [D, R8 * D])
        gin_w1 = [sb(f"gin_w1_{p}", [D, A[f"L0_gnn_w{p + 1}1"].shape[1]]) for p in GIN]
        gin_w2 = [sb(f"gin_w2_{p}", [A[f"L0_gnn_w{p + 1}2"].shape[0], D]) for p in GIN]
        gin_b1 = [sb(f"gin_b1_{p}", [A[f"L0_gnn_w{p + 1}1"].shape[1], 1]) for p in GIN]
        gin_b2 = [sb(f"gin_b2_{p}", [D, 1]) for p in GIN]
        root = [sb(f"root{n}", [D, D]) for n in range(2)]
        res_w = [sb(f"res_w{n}", [D, D]) for n in range(2)]
        rg_b = [sb(f"rg_b{n}", [D, 1]) for n in range(2)]
        res_b = [sb(f"res_b{n}", [D, 1]) for n in range(2)]
        gcn_w = sb("gcn_w", [D, D])
        gcn_wt = sb("gcn_wt", [D, D])
        gcn_b = sb("gcn_b", [BLK, D])
        prelu_a = sb("prelu_a", [BLK, 1])
        w_enc = sb("w_enc", [D, D])
        b_enc = sb("b_enc", [D, 1])
        w_self = sb("w_self", [D, D])
        rel_b = sb("rel_b", [D, 1])
        sum_ps = [pb("sum_ps0"), pb("sum_ps1")]
        aux_ps = [pb("aux_ps0"), pb("aux_ps1")]
        post_ps = pb("post_ps")
        tab_ps = [pb(f"tab_ps{n}") for n in range(3)]
        fm_a = post_ps[:, 0:BLK]
        fm_b = post_ps[:, 128:128 + BLK]
        nm_ps = post_ps[0:BLK, 256:256 + D]

        gathers = [(A["x"], src_i), (scratch["h1"], src_i), (scratch["h2"], src_i),
                   (scratch["t65a"], row_65), (scratch["t65b"], row_65), (scratch["hw"], src_i),
                   (scratch["t8"], row_8)]
        edge_scale = [edge_w, edge_w, edge_w, mean_w, mean_w, None, None]

        per_step = ("rows_staged", "summed", "hot_done", "added", "type_hot_done")
        per_block = {
            "in_done": (range(PASSES), 1), "stored": (range(PASSES), 16), "cleared": (range(6), 1),
            "hidden": (GIN, 1), "hidden_relu": (GIN, 1), "gin_out": (GIN, 1),
            "out_done": ((0, 1, 2, 5), 1), "out_turned": ((0, 1), 1), "rows_ready": ((0, 1, 4, 5, 6), 1),
            "y_done": ((2, 4, 5, 6), 1), "y_turned": ((2, 4, 6), 1), "stats": ((2, 4, 5, 6), 1),
            "moments": ((2, 4, 5, 6), 1), "std_done": ((2, 4, 5, 6), 1), "rstd": ((2, 4, 5, 6), 1),
            "z_done": ((2, 4, 5), 1), "z_turned": ((2, 4, 5), 1), "xblk_done": ((4, 5), 1),
            "parts_begun": ((2, 3), 1), "parts": ((2, 3), 3),
            "conv_mult": ((3, 4, 6), 1), "conv_sum": ((3, 4, 6), 1), "conv_relu": ((3, 4, 6), 1),
            "tab_act": ((2, 3), 5), "tab_dve": ((2, 3), 4)}

        def before(name, p, general):
            steps = SWEEPS * NG if general else NG
            if name in per_step:
                return p * steps
            if name == "staged":
                return sum(steps * (1 if edge_scale[q] is None else 2) for q in range(p))
            if name == "gathered":
                return p // 2 * steps // 2 * 16 * QUART
            if name == "tab_mult":
                return NB * sum({2: 9, 3: 9, 5: 1}.get(q, 0) for q in range(p))
            users, n = per_block[name]
            start = {"stored": 16, "cleared": 1}.get(name, 0)
            return start + NB * n * sum(q < p for q in users)

        def load_edges(eng, tile, src, done):
            full = (NG - 1) * GROUP
            t = tile[:, :].rearrange("p (g j) -> p g j", j=TILE)
            eng.dma_start(t[:, 0:NG - 1, :], src[0:full].rearrange("(g p j) -> p g j", p=128, j=TILE))\
               .then_inc(sem(done), 16)
            rows, rest = LAST // TILE, LAST % TILE
            eng.dma_start(t[0:rows, NG - 1, :],
                          src[full:full + rows * TILE].rearrange("(p j) -> p j", j=TILE))\
               .then_inc(sem(done), 16)
            eng.dma_start(t[rows:rows + 1, NG - 1, 0:rest],
                          src[full + rows * TILE:E].rearrange("(a j) -> a j", a=1))\
               .then_inc(sem(done), 16)

        small = [(gcn_w, A["L2_gnn_W"]), (w_enc, A["L3_gnn_W_enc"]), (w_self, A["L3_gnn_W_self"])]
        cols = [(b_enc, A["L3_gnn_b_enc"]), (rel_b, A["L3_gnn_bias"])]
        for p in GIN:
            small += [(gin_w1[p], A[f"L0_gnn_w{p + 1}1"]), (gin_w2[p], A[f"L0_gnn_w{p + 1}2"])]
            cols += [(gin_b1[p], A[f"L0_gnn_b{p + 1}1"]), (gin_b2[p], A[f"L0_gnn_b{p + 1}2"])]
        for n in range(2):
            small += [(root[n], A["L1_gnn_root"][n]), (res_w[n], A["L1_gnn_res_W"][n])]
            cols += [(rg_b[n], A["L1_gnn_bias"][n]), (res_b[n], A["L1_gnn_res_b"][n])]
        WEIGHTS = 16 * (len(small) + len(cols) + 2 + 1)

        def at(tile, n, w=1):
            return tile[:, n:n + w] if isinstance(n, int) else tile[:, bass.ds(n, w)]

        def cols_of(tile, b):
            return at(tile, b * BLK, BLK)

        def sums_of(b):
            return at(acc, b * BLK + SHIFT, BLK)

        def col16(tile, g):
            return at(tile, g * TILE, TILE)

        def nm_at(tile, b):
            return tile[:, b, :] if isinstance(b, int) else \
                tile[:, bass.ds(b, 1), :].rearrange("p a d -> p (a d)")

        def schedule(eng, general, turn, finish, setup=None):
            if general:
                with eng.Fori(0, SWEEPS) as k:
                    with eng.Fori(0, PAIRS) as i:
                        for u in range(2):
                            turn(k * NG + 2 * i + u, 2 * i + u, k, u, k * PAIRS + i, None)
                if setup:
                    setup()
                with eng.Fori(0, NB) as b:
                    for i in range(PHASES):
                        finish(i, b)
                return
            turn(0, 0, None, 0, 0, None)
            turn(1, 1, None, 1, 0, None)
            if setup:
                setup()
            with eng.Fori(1, PAIRS - 1) as i:
                for u in range(2):
                    s = 2 * i + u
                    turn(s, s, None, u, i, s - 2)
            turn(NG - 2, NG - 2, None, 0, PAIRS - 1, NG - 4)
            turn(NG - 1, NG - 1, None, 1, PAIRS - 1, NG - 3)

        def ahead(p, s):
            return (p + 1, 0) if isinstance(s, int) and s == NG - 1 else (p, s + 1)

        def by_branch(eng, run):
            eng.wait_ge(sem("flag_ready"), 1)
            general = eng.value_load(flag_i[0:1, 0:1], min_val=0, max_val=1)
            with eng.If(general == 0):
                run(False)
            with eng.Else():
                run(True)

        block = ctx.enter_context(nc.Block())

        @block.sync
        def _(sp):
            sp.wait_ge(sem("pads_set"), 5)
            load_edges(sp, dst_i, A["dst"], "dst_in")
            load_edges(sp, src_i, A["src"], "src_in")
            for tile, name in ((edge_w, "edge_weight"), (t65_i, "edge_type_65"), (t8_i, "edge_type_8")):
                load_edges(sp, tile, A[name], "edges_in")
            sp.dma_start(x_nm[:, :, :], A["x"].rearrange("(b p) d -> p b d", p=BLK))\
              .then_inc(sem("x_in"), 16)
            for tile, w in small:
                sp.dma_start(tile[:, :], w).then_inc(sem("weights_in"), 16)
            for tile, w in cols:
                sp.dma_start(tile[:, :], w.rearrange("(d a) -> d a", a=1)).then_inc(sem("weights_in"), 16)
            sp.dma_start(gcn_b[:, :], A["L2_gnn_b"].rearrange("(a d) -> a d", a=1).to_broadcast([BLK, D]))\
              .then_inc(sem("weights_in"), 16)
            sp.dma_start(prelu_a[:, :], A["L2_gnn_prelu_a"].rearrange("(a d) -> a d", a=1)
                         .to_broadcast([BLK, 1])).then_inc(sem("weights_in"), 16)
            sp.dma_start(w8[:, :].rearrange("d (r k) -> d r k", k=D),
                         A["L3_gnn_W_rel"].rearrange("r d k -> d r k")).then_inc(sem("weights_in"), 16)

            def load_w65(n):
                for half in range(2):
                    sp.dma_start(table_blk[half * D:(half + 1) * D, :].rearrange("d (r k) -> d r k", k=D),
                                 A["L1_gnn_W"][n].rearrange("r d k -> d r k")).then_inc(sem("w65_in"), 16)

            load_w65(0)
            sp.sem_inc(sem("stored"), 16)
            node_tables = {0: scratch["h1"], 1: scratch["h2"], 4: scratch["hw"], 6: out}
            wide_tables = {2: scratch["t65a"].rearrange("(n t) d -> n (t d)", t=R65),
                           3: scratch["t65b"].rearrange("(n t) d -> n (t d)", t=R65),
                           5: scratch["t8"].rearrange("(n t) d -> n (t d)", t=R8)}

            def rows(table, b):
                return table[b * BLK:(b + 1) * BLK, :] if isinstance(b, int) else \
                    table[bass.ds(b * BLK, BLK), :]

            def run(general):
                for p in range(PASSES):
                    if p == 3:
                        sp.wait_ge(sem("stored"), before("stored", p, general))
                        load_w65(1)
                    with sp.Fori(0, NB) as b:
                        if p in (2, 3):
                            sp.wait_ge(sem("tab_act"), before("tab_act", p, general) + 5 * b + 5)
                            sp.wait_ge(sem("tab_dve"), before("tab_dve", p, general) + 4 * b + 4)
                            sp.dma_start(rows(wide_tables[p], b), table_blk[0:BLK, :])\
                              .then_inc(sem("stored"), 16)
                        else:
                            sp.wait_ge(sem("rows_ready"), before("rows_ready", p, general) + b + 1)
                            if p == 5:
                                sp.dma_start(rows(wide_tables[p], b), table_blk[0:BLK, 0:R8 * D])\
                                  .then_inc(sem("stored"), 16)
                            else:
                                sp.dma_start(rows(node_tables[p], b),
                                             z_blk[:, 0, :] if p == REL else nm_blk[:, :])\
                                  .then_inc(sem("stored"), 16)
                sp.wait_ge(sem("stored"), before("stored", PASSES, general))

            by_branch(sp, run)

        @block.gpsimd
        def _(pool):
            last = slice((NG - 1) * TILE, NG * TILE)
            pool.memset(dst_i[:, last], N - 1).then_inc(sem("pads_set"), 1)
            pool.memset(src_i[:, last], 0).then_inc(sem("pads_set"), 1)
            pool.memset(t65_i[:, last], 0).then_inc(sem("pads_set"), 1)
            pool.memset(t8_i[:, last], 0).then_inc(sem("pads_set"), 1)
            pool.memset(edge_w[:, last], 0.0).then_inc(sem("pads_set"), 1)
            pool.memset(ones[:, :], 1.0).then_inc(sem("consts"), 1)
            pool.iota(group_base[:, :], pattern=[[STEP, NG]], base=0, channel_multiplier=0,
                      allow_small_or_imprecise_dtypes=True).then_inc(sem("consts"), 1)
            pool.iota(block_base[:, :], pattern=[[BLK, NG]], base=SHIFT - BLK, channel_multiplier=0,
                      allow_small_or_imprecise_dtypes=True).then_inc(sem("consts"), 1)
            pool.iota(sweep_base[:, :], pattern=[[WIN, SWEEPS]], base=0, channel_multiplier=0,
                      allow_small_or_imprecise_dtypes=True).then_inc(sem("consts"), 1)
            pool.iota(iota_win[:, :], pattern=[[1, WIN]], base=0, channel_multiplier=0,
                      allow_small_or_imprecise_dtypes=True).then_inc(sem("consts"), 1)
            pool.iota(iota_win_bf[:, :], pattern=[[1, WIN]], base=0, channel_multiplier=0,
                      allow_small_or_imprecise_dtypes=True).then_inc(sem("consts"), 1)
            pool.memset(last_mask[:, :], 1.0).then_inc(sem("masks_begun"), 1)
            pool.memset(ident[:, :], 0.0).then_inc(sem("masks_begun"), 1)
            pool.wait_ge(sem("masks_begun"), 2)
            pool.affine_select(out=last_mask[:, :], in_=last_mask[:, :], compare_op=ALU.is_ge, fill=0.0,
                               base=LAST - 1, pattern=[[-1, TILE]], channel_multiplier=-TILE)\
                .then_inc(sem("consts"), 1)
            pool.affine_select(out=ident[:, :], in_=ident[:, :], compare_op=ALU.not_equal, fill=1.0,
                               base=0, pattern=[[-1, 128]], channel_multiplier=1).then_inc(sem("consts"), 1)
            pool.iota(iota_type[:, :], pattern=[[0, TILE], [1, R65]], base=0, channel_multiplier=0,
                      allow_small_or_imprecise_dtypes=True).then_inc(sem("consts"), 1)

            def run(general):
                for p in range(PASSES):
                    table = gathers[p][0]
                    if p > 0:
                        pool.wait_ge(sem("stored"), before("stored", p, general))

                    def turn(s, g, k, u, n, b):
                        pool.wait_ge(sem("rows_staged"), before("rows_staged", p, general) + s + 1)
                        pool.sem_inc(sem("gather_begun"), 1)
                        for j in range(TILE):
                            pool.indirect_dma_start(
                                out=msgs[:, u, j, :], out_offset=None, in_=table[:, :],
                                in_offset=bass.IndirectOffsetOnAxis(ap=rows_now[:, u, j:j + 1], axis=0))\
                                .then_inc(sem("gathered", p % 2, u, j // QUART), 16)

                    schedule(pool, general, turn, lambda i, b: None)
                pool.wait_ge(sem("stored"), before("stored", PASSES, general))

            by_branch(pool, run)

        @block.scalar
        def _(act):
            act.wait_ge(sem("src_in"), 48)

            def run(general):
                def stage_rows(p, s, g, u):
                    act.wait_ge(sem("summed"), before("summed", p, general) + s + 1)
                    act.sem_inc(sem("act_turns"), 1)
                    act.activation(rows_now[:, u, :], col16(gathers[p][1], g), ACT.Copy)\
                       .then_inc(sem("rows_staged"), 1)

                if not general:
                    stage_rows(0, 0, 0, 0)
                for p in range(PASSES):
                    def turn(s, g, k, u, n, b):
                        if general:
                            stage_rows(p, s, g, u)
                        elif p < PASSES - 1 or not (isinstance(s, int) and s == NG - 1):
                            q, t = ahead(p, s)
                            stage_rows(q, t, t, 1 - u)
                        if b is not None:
                            finish(0, b)
                        if p == 1:
                            act.wait_ge(sem("summed"), before("summed", p, general) + s + 2)
                            for h in range(2):
                                act.wait_ge(sem("type_turned"), 2 * s + h + 1)
                                act.sem_inc(sem("act_turns"), 1)
                                act.activation(type_hot_t[:, 8 * h:8 * h + 8, :].rearrange("t j e -> t (j e)"),
                                               aux_ps[h][0:R65, :].bitcast(BF16), ACT.Copy)\
                                   .then_inc(sem("type_hot_t_done"), 1)
                        if b is not None:
                            for i in range(1, PHASES):
                                finish(i, b)

                    def root_of_variance(b):
                        act.wait_ge(sem("moments"), before("moments", p, general) + b + 1)
                        act.activation(std[:, :], mean_var[:, 1:2], ACT.Sqrt, bias=eps[0:BLK, :])\
                           .then_inc(sem("std_done"), 1)

                    def back(b):
                        act.wait_ge(sem("z_turned"), before("z_turned", p, general) + b + 1)
                        act.sem_inc(sem("act_turns"), 1)
                        act.activation(cols_of(x_fm, b), fm_a[0:D, :], ACT.Copy)
                        act.activation(xblk[:, :], fm_a[0:D, :], ACT.Copy).then_inc(sem("xblk_done"), 1)

                    def high_parts(b):
                        if p == 2:
                            act.wait_ge(sem("z_turned"), before("z_turned", p, general) + b + 1)
                            act.sem_inc(sem("act_turns"), 1)
                            act.activation(cols_of(x_fm, b), fm_a[0:D, :], ACT.Copy)
                        else:
                            act.wait_ge(sem("h_doubled"), b + 1)
                        act.activation(x_hi_mid[:, :], fm_a, ACT.Copy)
                        act.activation(x_hi_lo[:, :], fm_a, ACT.Copy).then_inc(sem("parts_begun"), 1)

                    def table(b):
                        act.wait_ge(sem("stored"), before("stored", p, general) + 16 * b)
                        for c in range(0, len(CHUNKS), 2):
                            o, w = CHUNKS[c]
                            act.wait_ge(sem("tab_mult"), before("tab_mult", p, general) + 9 * b + c + 1)
                            act.activation(table_blk[0:BLK, o:o + w], tab_ps[c % 3][0:BLK, 0:w], ACT.Copy)\
                               .then_inc(sem("tab_act"), 1)

                    def finish(i, b):
                        if p in GIN:
                            if i == 0:
                                f = gin_w1[p].shape[1]
                                act.wait_ge(sem("hidden"), before("hidden", p, general) + b + 1)
                                act.activation(hid_blk[0:f, :], fm_a[0:f, :], ACT.Relu, bias=gin_b1[p][:, :])\
                                   .then_inc(sem("hidden_relu"), 1)
                            elif i == 1:
                                act.wait_ge(sem("gin_out"), before("gin_out", p, general) + b + 1)
                                act.sem_inc(sem("act_turns"), 1)
                                if p < 2:
                                    act.activation(cols_of(h_fm, b), fm_b[0:D, :], ACT.Relu,
                                                   bias=gin_b2[p][:, :])
                                act.activation(out_blk[:, :], fm_b[0:D, :], ACT.Relu if p < 2 else ACT.Identity,
                                               bias=gin_b2[p][:, :]).then_inc(sem("out_done"), 1)
                            elif p == 2 and i == 2:
                                root_of_variance(b)
                            elif p == 2 and i == 3:
                                high_parts(b)
                            elif p == 2:
                                table(b)
                        elif p in RGCN:
                            if i == 0:
                                act.wait_ge(sem("conv_sum"), before("conv_sum", p, general) + b + 1)
                                act.activation(out_blk[:, :], y_blk[:, :], ACT.Relu, bias=rg_b[p - 3][:, :])
                                act.activation(res_blk[:, :], fm_b[0:D, :], ACT.Relu, bias=res_b[p - 3][:, :])\
                                   .then_inc(sem("conv_relu"), 1)
                            elif p == 3 and i == 1:
                                high_parts(b)
                            elif p == 3 and i == 4:
                                table(b)
                            elif p == 4 and i == 2:
                                root_of_variance(b)
                            elif p == 4 and i == 3:
                                back(b)
                        elif p == GCN:
                            if i == 0:
                                root_of_variance(b)
                            elif i == 1:
                                back(b)
                            elif i == 2:
                                act.wait_ge(sem("encoded"), b + 1)
                                act.sem_inc(sem("act_turns"), 1)
                                act.activation(cols_of(h_fm, b), fm_b[0:D, :], ACT.Relu, bias=b_enc[:, :])
                                act.activation(out_blk[:, :], fm_b[0:D, :], ACT.Relu, bias=b_enc[:, :])\
                                   .then_inc(sem("out_done"), 1)
                            elif i == 3:
                                act.wait_ge(sem("stored"), before("stored", p, general) + 16 * b)
                                act.wait_ge(sem("tab_mult"), before("tab_mult", p, general) + b + 1)
                                act.activation(table_blk[0:BLK, 0:R8 * D], tab_ps[0][0:BLK, 0:R8 * D],
                                               ACT.Copy).then_inc(sem("rows_ready"), 1)
                        else:
                            if i == 0:
                                act.wait_ge(sem("conv_sum"), before("conv_sum", p, general) + b + 1)
                                act.activation(out_blk[:, :], y_blk[:, :], ACT.Relu, bias=rel_b[:, :])\
                                   .then_inc(sem("conv_relu"), 1)
                            elif i == 2:
                                root_of_variance(b)

                    def setup():
                        if p == 0:
                            for n in range(XBANKS):
                                w = min(4, NB - 4 * n) * BLK
                                act.wait_ge(sem("x_turned"), n + 1)
                                act.activation(x_fm[:, 4 * n * BLK:4 * n * BLK + w], tab_ps[n % 3][0:D, 0:w],
                                               ACT.Copy).then_inc(sem("x_fm_done"), 1)
                            act.wait_ge(sem("gcn_w_turned"), 1)
                            act.activation(gcn_wt[:, :], post_ps[0:D, 0:D], ACT.Copy)\
                               .then_inc(sem("gcn_wt_done"), 1)
                        layer = p // 3
                        act.wait_ge(sem("w65_in"), 32 * (layer + 1))
                        if p == 3:
                            act.wait_ge(sem("tab_mult"), before("tab_mult", p, general))
                        act.activation(w_hi[:, :], table_blk[:, :], ACT.Copy).then_inc(sem("w_high"), 1)
                        act.wait_ge(sem("w_high"), layer + 1)
                        act.activation(w_lo_hi[D:128, :], w_hi[D:128, :], ACT.Copy).then_inc(sem("w_high_again"), 1)
                        act.wait_ge(sem("w_rest"), layer + 1)
                        act.activation(w_mid[:, :], table_blk[:, :], ACT.Copy).then_inc(sem("w_middle"), 1)

                    schedule(act, general, turn, finish, setup if p in (0, 3) else None)
                    if not general:
                        for i in range(PHASES):
                            finish(i, NB - 1)
                    if p == 0:
                        act.wait_ge(sem("degrees"), 1)
                        act.activation(dinv[:, :], aux_ps[0][0:BLK, 0:NB], ACT.Sqrt, bias=ones[0:BLK, :])\
                           .then_inc(sem("degree_root"), 1)

            by_branch(act, run)

        @block.tensor
        def _(pe):
            pe.wait_ge(sem("consts"), 9)
            pe.sem_inc(sem("summed"), 2)
            pe.wait_ge(sem("outside_done"), 1)
            pe.matmul(post_ps[0:1, 0:1], flag_f[:, :], ones[:, :]).then_inc(sem("outside_sum"), 1)

            def run(general):
                for p in range(PASSES):
                    def turn_types(s):
                        pe.wait_ge(sem("type_hot_done"), before("type_hot_done", p, general) + s + 1)
                        pe.sem_inc(sem("pe_turns"), 1)
                        for j in range(TILE):
                            bank = aux_ps[j // 8][0:R65, :].bitcast(BF16)
                            last = pe.transpose(bank[:, (j % 8) * 128:(j % 8 + 1) * 128],
                                                type_hot[:, j, :], ident_bf[:, :])
                            if j % 8 == 7:
                                last.then_inc(sem("type_turned"), 1)

                    def look_up(i, s):
                        for j in range(QUART * i, QUART * (i + 1)):
                            if j == 0:
                                pe.wait_ge(sem("inv_parts"), 4 * s + 4)
                            if j % 8 == 0:
                                pe.wait_ge(sem("type_hot_t_done"), 2 * s + j // 8 + 1)
                            if j % 2 == 0:
                                pe.wait_ge(sem("look_used"), TILE // 2 * s + j // 2 + 1)
                                pe.sem_inc(sem("pe_turns"), 1)
                            for part in range(3):
                                last = pe.matmul(tab_ps[j // 2 % 2][:, (j % 2) * WIN:(j % 2 + 1) * WIN],
                                                 type_hot_t[:, j, :], inv_now[:, part, :],
                                                 start=(part == 0), stop=(part == 2))
                            if j % 2:
                                last.then_inc(sem("look_done"), 1)

                    def sum_up(i, s, u, n):
                        if i == 0:
                            pe.wait_ge(sem("hot_done"), before("hot_done", p, general) + s + 1)
                        pe.wait_ge(sem("gathered", p % 2, u, i),
                                   before("gathered", p, general) + 16 * QUART * (n + 1))
                        for j in range(QUART * i, QUART * (i + 1)):
                            last = pe.matmul(sum_ps[u][0:D, 0:WIN], msgs[:, u, j, :], hot[:, u, j, :],
                                             start=(j == 0), stop=(j == TILE - 1))
                        if i == 3:
                            last.then_inc(sem("summed"), 1)

                    def turn(s, g, k, u, n, b):
                        if b is not None:
                            finish(0, b)
                        if p == 0:
                            pe.wait_ge(sem("type_hot_done"), s + 1)
                            for j in range(TILE):
                                pe.matmul(aux_ps[u][0:R65, 0:WIN], type_hot[:, j, :], hot_bf[:, j, :],
                                          start=(j == 0), stop=(j == TILE - 1))
                        if p == 1:
                            turn_types(s)
                        for i in range(4):
                            if p == 1:
                                look_up(i, s)
                            sum_up(i, s, u, n)
                            if b is not None:
                                finish(i + 1, b)

                    def turn_y(b):
                        pe.wait_ge(sem("y_done"), before("y_done", p, general) + b + 1)
                        pe.sem_inc(sem("pe_turns"), 1)
                        pe.transpose(nm_ps, y_blk[:, :], ident[0:D, 0:D]).then_inc(sem("y_turned"), 1)

                    def turn_z(b):
                        pe.wait_ge(sem("z_done"), before("z_done", p, general) + b + 1)
                        pe.sem_inc(sem("pe_turns"), 1)
                        if p == 2:
                            pe.transpose(fm_a, z_blk[:, :, :].rearrange("n a d -> n (a d)"),
                                         ident[0:BLK, 0:BLK]).then_inc(sem("z_turned"), 1)
                        else:
                            pe.transpose(fm_a[0:D, :], z_blk[:, 0, :], ident[0:BLK, 0:BLK])\
                              .then_inc(sem("z_turned"), 1)

                    def table(b):
                        pe.wait_ge(sem("parts"), before("parts", p, general) + 3 * b + 3)
                        pe.sem_inc(sem("pe_turns"), 1)
                        for c, (o, w) in enumerate(CHUNKS):
                            if c >= 3:
                                if c % 2:
                                    pe.wait_ge(sem("tab_act"), before("tab_act", p, general) + 5 * b + (c - 3) // 2 + 1)
                                else:
                                    pe.wait_ge(sem("tab_dve"), before("tab_dve", p, general) + 4 * b + (c - 3) // 2 + 1)
                                pe.sem_inc(sem("pe_turns"), 1)
                            products = ((x_hi_mid, w_hi), (x_hi_mid, w_mid), (x_hi_lo, w_lo_hi))
                            for n, (x_part, w_part) in enumerate(products):
                                last = pe.matmul(tab_ps[c % 3][0:BLK, 0:w], x_part[:, :], w_part[:, o:o + w],
                                                 start=(n == 0), stop=(n == 2))
                            last.then_inc(sem("tab_mult"), 1)

                    def finish(i, b):
                        if p in GIN:
                            f = gin_w1[p].shape[1]
                            if i == 0:
                                pe.wait_ge(sem("in_done"), before("in_done", p, general) + b + 1)
                                pe.sem_inc(sem("pe_turns"), 1)
                                pe.matmul(fm_a[0:f, :], gin_w1[p][:, :], in_blk[:, :]).then_inc(sem("hidden"), 1)
                            elif i == 1:
                                pe.wait_ge(sem("hidden_relu"), before("hidden_relu", p, general) + b + 1)
                                pe.sem_inc(sem("pe_turns"), 1)
                                pe.matmul(fm_b[0:D, :], gin_w2[p][:, :], hid_blk[0:f, :])\
                                  .then_inc(sem("gin_out"), 1)
                            elif p < 2 and i == 2:
                                pe.wait_ge(sem("out_done"), before("out_done", p, general) + b + 1)
                                pe.sem_inc(sem("pe_turns"), 1)
                                pe.transpose(nm_ps, out_blk[:, :], ident[0:D, 0:D])\
                                  .then_inc(sem("out_turned"), 1)
                            elif p == 2 and i == 2:
                                turn_y(b)
                            elif p == 2 and i == 3:
                                turn_z(b)
                            elif p == 2:
                                table(b)
                        elif p in RGCN:
                            if i == 0:
                                pe.wait_ge(sem("in_done"), before("in_done", p, general) + b + 1)
                                pe.sem_inc(sem("pe_turns"), 1)
                                pe.matmul(fm_a[0:D, :], root[p - 3][:, :], in_blk[:, :])
                                pe.matmul(fm_b[0:D, :], res_w[p - 3][:, :], in_blk[:, :])\
                                  .then_inc(sem("conv_mult"), 1)
                            elif p == 3 and i == 1:
                                pe.wait_ge(sem("h_done"), b + 1)
                                pe.sem_inc(sem("pe_turns"), 1)
                                pe.matmul(fm_a, ident_twice[:, :, :].rearrange("d a k -> d (a k)"), xblk[:, :])\
                                  .then_inc(sem("h_doubled"), 1)
                            elif p == 3 and i == 4:
                                table(b)
                            elif p == 4 and i == 2:
                                turn_y(b)
                            elif p == 4 and i == 3:
                                turn_z(b)
                            elif p == 4 and i == 4:
                                pe.wait_ge(sem("xblk_done"), before("xblk_done", p, general) + b + 1)
                                pe.sem_inc(sem("pe_turns"), 1)
                                pe.matmul(nm_ps, xblk[:, :], gcn_wt[:, :]).then_inc(sem("gcn_mult"), 1)
                        elif p == GCN:
                            if i == 0:
                                pe.wait_ge(sem("in_done"), before("in_done", p, general) + b + 1)
                                pe.sem_inc(sem("pe_turns"), 1)
                                pe.transpose(nm_ps, in_blk[:, :], ident[0:D, 0:D])\
                                  .then_inc(sem("sum_turned"), 1)
                            elif i == 1:
                                turn_z(b)
                            elif i == 2:
                                pe.wait_ge(sem("xblk_done"), before("xblk_done", p, general) + b + 1)
                                pe.sem_inc(sem("pe_turns"), 1)
                                pe.matmul(fm_b[0:D, :], w_enc[:, :], xblk[:, :]).then_inc(sem("encoded"), 1)
                            elif i == 3:
                                pe.wait_ge(sem("out_done"), before("out_done", p, general) + b + 1)
                                pe.sem_inc(sem("pe_turns"), 1)
                                pe.matmul(tab_ps[0][0:BLK, 0:R8 * D], out_blk[:, :], w8[:, :])\
                                  .then_inc(sem("tab_mult"), 1)
                        else:
                            if i == 0:
                                pe.wait_ge(sem("in_done"), before("in_done", p, general) + b + 1)
                                pe.sem_inc(sem("pe_turns"), 1)
                                pe.matmul(fm_a[0:D, :], w_self[:, :], in_blk[:, :]).then_inc(sem("conv_mult"), 1)
                            elif i == 1:
                                turn_y(b)

                    def setup():
                        if p == 3:
                            pe.wait_ge(sem("w_split"), 2)
                            return
                        pe.wait_ge(sem("x_in"), 16)
                        for n in range(XBANKS):
                            if n >= 3:
                                pe.wait_ge(sem("x_fm_done"), n - 2)
                            for b in range(4 * n, min(4 * n + 4, NB)):
                                o = (b % 4) * BLK
                                last = pe.transpose(tab_ps[n % 3][0:D, o:o + BLK], x_nm[:, b, :],
                                                    ident[0:BLK, 0:BLK])
                            last.then_inc(sem("x_turned"), 1)
                        pe.wait_ge(sem("weights_in"), WEIGHTS)
                        pe.transpose(post_ps[0:D, 0:D], gcn_w[:, :], ident[0:D, 0:D])\
                          .then_inc(sem("gcn_w_turned"), 1)
                        pe.wait_ge(sem("gcn_wt_done"), 1)

                    if p == 2:
                        pe.wait_ge(sem("w_split"), 1)
                    schedule(pe, general, turn, finish, setup if p in (0, 3) else None)
                    if not general:
                        for i in range(PHASES):
                            finish(i, NB - 1)
                    if p == 0:
                        pe.wait_ge(sem("counts_done"), SWEEPS * NG if general else NG)
                        for b in range(NB):
                            o = SHIFT + b * BLK
                            last = pe.matmul(aux_ps[0][0:BLK, b:b + 1], counts[:, o:o + BLK], ones[0:R65, :])
                        last.then_inc(sem("degrees"), 1)

            by_branch(pe, run)

        @block.vector
        def _(dve):
            dve.memset(acc[:, :], 0.0).then_inc(sem("cleared"), 1)
            dve.memset(counts[:, :], 0.0).then_inc(sem("fills"), 1)
            dve.memset(mean_w[:, :], 0.0).then_inc(sem("fills"), 1)
            dve.memset(zeros[:, :], 0.0).then_inc(sem("fills"), 1)
            dve.memset(eps[:, :], EPS).then_inc(sem("fills"), 1)
            dve.wait_ge(sem("consts"), 9)
            dve.wait_ge(sem("dst_in"), 48)
            dve.tensor_scalar(slot_f[:, :], dst_i[:, :], float(SHIFT), None, ALU.add).then_inc(sem("prep"), 1)
            dve.wait_ge(sem("prep"), 1)
            for above, base in ((above_window, group_base), (above_block, block_base)):
                dve.tensor_tensor(above[:, :].rearrange("p (g j) -> p g j", j=TILE),
                                  slot_f[:, :].rearrange("p (g j) -> p g j", j=TILE),
                                  base[:, :].unsqueeze(2).to_broadcast([128, NG, TILE]), ALU.subtract)\
                   .then_inc(sem("prep"), 1)
            dve.wait_ge(sem("prep"), 3)
            dve.tensor_reduce(worst[:, 0:1], above_window[:, :], AX.X, ALU.max).then_inc(sem("prep"), 1)
            dve.tensor_reduce(worst[:, 1:2], above_window[:, :], AX.X, ALU.min).then_inc(sem("prep"), 1)
            dve.tensor_reduce(worst[:, 2:3], above_block[:, :], AX.X, ALU.min).then_inc(sem("prep"), 1)
            dve.wait_ge(sem("prep"), 6)
            dve.tensor_scalar(worst[:, 0:1], worst[:, 0:1], float(WIN - 1), None, ALU.is_gt)\
               .then_inc(sem("prep"), 1)
            dve.tensor_scalar(worst[:, 1:3], worst[:, 1:3], 0.0, None, ALU.is_lt).then_inc(sem("prep"), 1)
            dve.wait_ge(sem("prep"), 8)
            dve.tensor_reduce(flag_f[:, :], worst[:, :], AX.X, ALU.max).then_inc(sem("outside_done"), 1)
            lastg = slot_f[:, (NG - 1) * TILE:NG * TILE]
            dve.scalar_tensor_tensor(out=lastg, in0=lastg, scalar=NOWHERE, in1=last_mask[:, :],
                                     op0=ALU.add, op1=ALU.mult).then_inc(sem("prep"), 1)
            dve.wait_ge(sem("prep"), 9)
            dve.tensor_scalar(lastg, lastg, -NOWHERE, None, ALU.add).then_inc(sem("prep"), 1)
            dve.wait_ge(sem("outside_sum"), 1)
            dve.tensor_scalar(flag_i[:, :], post_ps[0:1, 0:1], 0.5, None, ALU.is_gt)\
               .then_inc(sem("flag_ready"), 1)
            dve.tensor_copy(ident_bf[:, :], ident[:, :]).then_inc(sem("prep"), 1)
            dve.tensor_copy(ident_twice[:, :, :], ident[0:D, 0:D].unsqueeze(1).to_broadcast([D, 2, D]))\
               .then_inc(sem("prep"), 1)
            dve.wait_ge(sem("src_in"), 48)
            dve.wait_ge(sem("edges_in"), 9 * 16)
            dve.tensor_copy(t65_f[:, :], t65_i[:, :]).then_inc(sem("prep"), 1)
            dve.scalar_tensor_tensor(out=row_65[:, :], in0=src_i[:, :], scalar=float(R65),
                                     in1=t65_i[:, :], op0=ALU.mult, op1=ALU.add).then_inc(sem("prep"), 1)
            dve.scalar_tensor_tensor(out=row_8[:, :], in0=src_i[:, :], scalar=float(R8),
                                     in1=t8_i[:, :], op0=ALU.mult, op1=ALU.add).then_inc(sem("prep"), 1)
            dve.wait_ge(sem("prep"), 15)
            dve.wait_ge(sem("fills"), 4)
            dve.sem_inc(sem("look_used"), 2)

            def run(general):
                def one_hots(p, s, g, k, u):
                    scale = edge_scale[p]
                    dve.wait_ge(sem("summed"), before("summed", p, general) + s + 1)
                    base = at(sweep_base, k) if general else at(group_base, g)
                    dve.tensor_scalar(rel_now[:, u, :], col16(slot_f, g), base, None, ALU.subtract)\
                       .then_inc(sem("staged"), 1)
                    if scale is not None:
                        dve.tensor_copy(w_now[:, u, :], col16(scale, g)).then_inc(sem("staged"), 1)
                    dve.wait_ge(sem("staged"), before("staged", p, general)
                                + (s + 1) * (1 if scale is None else 2))
                    for j in range(TILE):
                        if scale is None:
                            last = dve.tensor_scalar(hot[:, u, j, :], iota_win[:, :],
                                                     rel_now[:, u, j:j + 1], None, ALU.is_equal)
                        else:
                            last = dve.tensor_scalar(hot[:, u, j, :], iota_win[:, :],
                                                     rel_now[:, u, j:j + 1], w_now[:, u, j:j + 1],
                                                     ALU.is_equal, ALU.mult)
                    last.then_inc(sem("hot_done"), 1)

                if not general:
                    one_hots(0, 0, 0, None, 0)
                for p in range(PASSES):
                    def add_sums(s, base, u):
                        dve.wait_ge(sem("summed"), before("summed", p, general) + s + 3)
                        dve.tensor_tensor(at(acc, base, WIN), at(acc, base, WIN), sum_ps[u][0:D, 0:WIN],
                                          ALU.add).then_inc(sem("added"), 1)
                        if p == 0:
                            dve.tensor_tensor(at(counts, base, WIN), at(counts, base, WIN),
                                              aux_ps[u][0:R65, 0:WIN], ALU.add)\
                               .then_inc(sem("counts_done"), 1)
                            dve.wait_ge(sem("counts_done"), s + 1)
                        dve.wait_ge(sem("added"), before("added", p, general) + s + 1)
                        dve.sem_inc(sem("dve_turns"), 1)

                    def type_one_hots(g):
                        dve.tensor_tensor(
                            type_hot[:, :, :], iota_type[:, :].rearrange("p (j t) -> p j t", t=R65),
                            col16(t65_f, g).unsqueeze(2).to_broadcast([128, TILE, R65]), ALU.is_equal)\
                           .then_inc(sem("type_hot_done"), 1)

                    def count_one_hots(s, g, u):
                        dve.wait_ge(sem("summed"), before("summed", p, general) + s + 2)
                        for j in range(TILE):
                            dve.tensor_scalar(hot_bf[:, j, :], iota_win_bf[:, :], rel_now[:, u, j:j + 1],
                                              None, ALU.is_equal)
                        type_one_hots(g)

                    def start_look_up(s, g, k):
                        dve.wait_ge(sem("summed"), before("summed", p, general) + s + 2)
                        type_one_hots(g)
                        window = at(counts, k * WIN if general else g * STEP, WIN)
                        dve.tensor_copy(inv_now[:, 0, :], window).then_inc(sem("inv_parts"), 1)
                        dve.wait_ge(sem("inv_parts"), 4 * s + 1)
                        dve.tensor_tensor(inv_rest[:, :], window, inv_now[:, 0, :], ALU.subtract)\
                           .then_inc(sem("inv_parts"), 1)
                        dve.wait_ge(sem("inv_parts"), 4 * s + 2)
                        dve.tensor_copy(inv_now[:, 1, :], inv_rest[:, :]).then_inc(sem("inv_parts"), 1)
                        dve.wait_ge(sem("inv_parts"), 4 * s + 3)
                        dve.tensor_tensor(inv_now[:, 2, :], inv_rest[:, :], inv_now[:, 1, :], ALU.subtract)\
                           .then_inc(sem("inv_parts"), 1)

                    def look_up(i, s, u):
                        for j in range(QUART * i, QUART * (i + 1)):
                            if j % 2 == 0:
                                dve.wait_ge(sem("look_done"), TILE // 2 * s + j // 2 + 1)
                            last = dve.scalar_tensor_tensor(
                                out=junk[:, j % 4, :], in0=iota_win[:, :], scalar=rel_now[:, u, j:j + 1],
                                in1=tab_ps[j // 2 % 2][:, (j % 2) * WIN:(j % 2 + 1) * WIN],
                                op0=ALU.is_equal, op1=ALU.mult, accum_out=mean_now[:, j:j + 1])
                            if j % 2:
                                last.then_inc(sem("look_used"), 1)

                    def end_look_up(s, g):
                        dve.wait_ge(sem("look_used"), TILE // 2 * s + TILE // 2 + 2)
                        dve.tensor_tensor(col16(mean_w, g), col16(mean_w, g), mean_now[:, :], ALU.add)\
                           .then_inc(sem("mean_w_done"), 1)
                        dve.wait_ge(sem("mean_w_done"), s + 1)

                    def turn(s, g, k, u, n, b):
                        if general:
                            one_hots(p, s, g, k, u)
                        elif b is not None or s == 1:
                            add_last(s, 1 - u)
                        if p == 0:
                            count_one_hots(s, g, u)
                        if p == 1:
                            start_look_up(s, g, k)
                        if b is not None:
                            finish(0, b)
                        if not general and (p < PASSES - 1 or not (isinstance(s, int) and s == NG - 1)):
                            q, t = ahead(p, s)
                            one_hots(q, t, t, None, 1 - u)
                        for i in range(4):
                            if p == 1:
                                look_up(i, s, u)
                                if i == 3:
                                    end_look_up(s, g)
                            if b is not None:
                                finish(i + 1, b)
                        if general:
                            add_sums(s, k * WIN, u)

                    def add_last(s, u):
                        if isinstance(s, int) and s == 1:
                            dve.wait_ge(sem("cleared"), before("cleared", p, general))
                        elif p == REL:
                            dve.wait_ge(sem("conv_sum"), before("conv_sum", p, general) + s - 2)
                        else:
                            dve.wait_ge(sem("cleared"), before("cleared", p, general) + s - 2)
                        add_sums(s - 1, (s - 1) * STEP, u)

                    def clear(b):
                        dve.tensor_copy(sums_of(b), zeros[:, :]).then_inc(sem("cleared"), 1)

                    def norm(b, y):
                        dve.bn_stats(stats[:, :], y).then_inc(sem("stats"), 1)
                        dve.wait_ge(sem("stats"), before("stats", p, general) + b + 1)
                        dve.sem_inc(sem("dve_turns"), 1)
                        dve.bn_aggr(mean_var[:, :], stats[:, :]).then_inc(sem("moments"), 1)
                        dve.wait_ge(sem("std_done"), before("std_done", p, general) + b + 1)
                        dve.reciprocal(rstd[:, :], std[:, :]).then_inc(sem("rstd"), 1)
                        dve.wait_ge(sem("rstd"), before("rstd", p, general) + b + 1)
                        if p == 2:
                            dve.tensor_scalar(z_blk[:, 1, :], y, mean_var[:, 0:1], rstd[:, :],
                                              ALU.subtract, ALU.mult)
                        if p == 4:
                            dve.tensor_scalar(nm_at(x_nm, b), y, mean_var[:, 0:1], rstd[:, :],
                                              ALU.subtract, ALU.mult)
                        if p == REL:
                            dve.wait_ge(sem("stored"), before("stored", p, general) + 16 * b)
                        dve.tensor_scalar(z_blk[:, 0, :], y, mean_var[:, 0:1], rstd[:, :],
                                          ALU.subtract, ALU.mult)\
                           .then_inc(sem("rows_ready" if p == REL else "z_done"), 1)

                    def low_parts(b):
                        done = before("parts", p, general) + 3 * b
                        dve.wait_ge(sem("parts_begun"), before("parts_begun", p, general) + b + 1)
                        dve.tensor_tensor(x_rest[D:128, :], fm_a[D:128, :], x_hi_mid[D:128, :], ALU.subtract)\
                           .then_inc(sem("parts"), 1)
                        dve.wait_ge(sem("parts"), done + 1)
                        dve.tensor_copy(x_hi_mid[D:128, :], x_rest[D:128, :]).then_inc(sem("parts"), 1)
                        dve.wait_ge(sem("parts"), done + 2)
                        dve.tensor_tensor(x_hi_lo[D:128, :], x_rest[D:128, :], x_hi_mid[D:128, :], ALU.subtract)\
                           .then_inc(sem("parts"), 1)

                    def table(b):
                        dve.wait_ge(sem("stored"), before("stored", p, general) + 16 * b)
                        for c in range(1, len(CHUNKS), 2):
                            o, w = CHUNKS[c]
                            dve.wait_ge(sem("tab_mult"), before("tab_mult", p, general) + 9 * b + c + 1)
                            dve.tensor_copy(table_blk[0:BLK, o:o + w], tab_ps[c % 3][0:BLK, 0:w])\
                               .then_inc(sem("tab_dve"), 1)

                    def conv_start(b, source):
                        dve.tensor_copy(in_blk[:, :], cols_of(source, b)).then_inc(sem("in_done"), 1)
                        dve.wait_ge(sem("conv_mult"), before("conv_mult", p, general) + b + 1)
                        dve.tensor_tensor(y_blk[:, :], fm_a[0:D, :], sums_of(b), ALU.add)\
                           .then_inc(sem("conv_sum"), 1)

                    def finish(i, b):
                        if p in GIN:
                            if i == 0:
                                dve.tensor_tensor(in_blk[:, :], sums_of(b),
                                                  cols_of(x_fm if p == 0 else h_fm, b), ALU.add)\
                                   .then_inc(sem("in_done"), 1)
                            elif p < 2 and i == 2:
                                dve.wait_ge(sem("out_turned"), before("out_turned", p, general) + b + 1)
                                dve.wait_ge(sem("stored"), before("stored", p, general) + 16 * b)
                                dve.tensor_copy(nm_blk[:, :], nm_ps).then_inc(sem("rows_ready"), 1)
                                clear(b)
                            elif p == 2 and i == 1:
                                dve.wait_ge(sem("out_done"), before("out_done", p, general) + b + 1)
                                dve.tensor_tensor(y_blk[:, :], out_blk[:, :], cols_of(x_fm, b), ALU.add)\
                                   .then_inc(sem("y_done"), 1)
                                clear(b)
                            elif p == 2 and i == 2:
                                dve.wait_ge(sem("y_turned"), before("y_turned", p, general) + b + 1)
                                norm(b, nm_ps)
                            elif p == 2 and i == 3:
                                low_parts(b)
                            elif p == 2:
                                table(b)
                        elif p == 3:
                            if i == 0:
                                conv_start(b, x_fm)
                            elif i == 1:
                                dve.wait_ge(sem("conv_relu"), before("conv_relu", p, general) + b + 1)
                                dve.tensor_tensor(cols_of(h_fm, b), out_blk[:, :], res_blk[:, :], ALU.add)
                                dve.tensor_tensor(xblk[:, :], out_blk[:, :], res_blk[:, :], ALU.add)\
                                   .then_inc(sem("h_done"), 1)
                                clear(b)
                            elif i == 2:
                                low_parts(b)
                            elif i == 4:
                                table(b)
                        elif p == 4:
                            if i == 0:
                                conv_start(b, h_fm)
                            elif i == 1:
                                dve.wait_ge(sem("conv_relu"), before("conv_relu", p, general) + b + 1)
                                dve.tensor_tensor(res_blk[:, :], out_blk[:, :], res_blk[:, :], ALU.add)\
                                   .then_inc(sem("h2_done"), 1)
                                clear(b)
                                dve.wait_ge(sem("h2_done"), b + 1)
                                dve.tensor_tensor(y_blk[:, :], res_blk[:, :], cols_of(x_fm, b), ALU.add)\
                                   .then_inc(sem("y_done"), 1)
                            elif i == 2:
                                dve.wait_ge(sem("y_turned"), before("y_turned", p, general) + b + 1)
                                norm(b, nm_ps)
                            elif i == 4:
                                dve.wait_ge(sem("gcn_mult"), b + 1)
                                dve.tensor_scalar(nm_at(hws_nm, b), nm_ps, at(dinv, b), None, ALU.mult)
                                dve.wait_ge(sem("stored"), before("stored", p, general) + 16 * b)
                                dve.tensor_scalar(nm_blk[:, :], nm_ps, at(dinv, b), None, ALU.mult)\
                                   .then_inc(sem("rows_ready"), 1)
                        elif p == GCN:
                            if i > 0:
                                return
                            dve.tensor_copy(in_blk[:, :], sums_of(b)).then_inc(sem("in_done"), 1)
                            dve.wait_ge(sem("sum_turned"), b + 1)
                            dve.tensor_tensor(y_nm[:, :], nm_ps, nm_at(hws_nm, b), ALU.add)\
                               .then_inc(sem("gcn_steps"), 1)
                            clear(b)
                            dve.wait_ge(sem("gcn_steps"), 4 * b + 1)
                            dve.scalar_tensor_tensor(out=y_nm[:, :], in0=y_nm[:, :], scalar=at(dinv, b),
                                                     in1=gcn_b[:, :], op0=ALU.mult, op1=ALU.add)\
                               .then_inc(sem("gcn_steps"), 1)
                            dve.wait_ge(sem("gcn_steps"), 4 * b + 2)
                            dve.tensor_scalar(neg_nm[:, :], y_nm[:, :], 0.0, prelu_a[:, :], ALU.min, ALU.mult)\
                               .then_inc(sem("gcn_steps"), 1)
                            dve.wait_ge(sem("gcn_steps"), 4 * b + 3)
                            dve.scalar_tensor_tensor(out=y_nm[:, :], in0=y_nm[:, :], scalar=0.0,
                                                     in1=neg_nm[:, :], op0=ALU.max, op1=ALU.add)\
                               .then_inc(sem("gcn_steps"), 1)
                            dve.wait_ge(sem("gcn_steps"), 4 * b + 4)
                            dve.tensor_tensor(y_nm[:, :], y_nm[:, :], nm_at(x_nm, b), ALU.add)\
                               .then_inc(sem("y_done"), 1)
                            dve.wait_ge(sem("y_done"), before("y_done", p, general) + b + 1)
                            norm(b, y_nm[:, :])
                        else:
                            if i == 0:
                                conv_start(b, h_fm)
                            elif i == 1:
                                dve.wait_ge(sem("conv_relu"), before("conv_relu", p, general) + b + 1)
                                dve.tensor_tensor(res_blk[:, :], out_blk[:, :], cols_of(h_fm, b), ALU.add)\
                                   .then_inc(sem("h_sum"), 1)
                                dve.wait_ge(sem("h_sum"), b + 1)
                                dve.tensor_tensor(y_blk[:, :], res_blk[:, :], cols_of(x_fm, b), ALU.add)\
                                   .then_inc(sem("y_done"), 1)
                            elif i == 2:
                                dve.wait_ge(sem("y_turned"), before("y_turned", p, general) + b + 1)
                                norm(b, nm_ps)

                    def setup():
                        if p == 0:
                            dve.wait_ge(sem("x_fm_done"), XBANKS)
                            dve.wait_ge(sem("weights_in"), WEIGHTS)
                        layer = p // 3
                        dve.wait_ge(sem("w_high"), layer + 1)
                        dve.tensor_tensor(table_blk[:, :], table_blk[:, :], w_hi[:, :], ALU.subtract)\
                           .then_inc(sem("w_rest"), 1)
                        dve.wait_ge(sem("w_middle"), layer + 1)
                        dve.tensor_tensor(w_lo_hi[0:D, :], table_blk[0:D, :], w_mid[0:D, :], ALU.subtract)\
                           .then_inc(sem("w_split"), 1)

                    if general and p > 0:
                        dve.wait_ge(sem("cleared"), before("cleared", p, general))
                    schedule(dve, general, turn, finish, setup if p in (0, 3) else None)
                    if not general:
                        add_last(NG, 1)
                        for i in range(PHASES):
                            finish(i, NB - 1)
                    if p == 0:
                        dve.wait_ge(sem("degree_root"), 1)
                        dve.reciprocal(dinv[:, :], dinv[:, :]).then_inc(sem("dinv_done"), 1)
                        dve.tensor_scalar(counts[:, :], counts[:, :], 1.0, None, ALU.max)\
                           .then_inc(sem("counts_max"), 1)
                        dve.wait_ge(sem("counts_max"), 1)
                        dve.reciprocal(counts[:, :], counts[:, :]).then_inc(sem("inverse_done"), 1)
                        dve.wait_ge(sem("inverse_done"), 1)

            by_branch(dve, run)


_INS = ["x", "src", "dst", "edge_type_65", "edge_type_8", "edge_weight",
        "L0_gnn_w11", "L0_gnn_b11", "L0_gnn_w12", "L0_gnn_b12", "L0_gnn_w21", "L0_gnn_b21",
        "L0_gnn_w22", "L0_gnn_b22", "L0_gnn_w31", "L0_gnn_b31", "L0_gnn_w32", "L0_gnn_b32",
        "L1_gnn_W", "L1_gnn_root", "L1_gnn_bias", "L1_gnn_res_W", "L1_gnn_res_b",
        "L2_gnn_W", "L2_gnn_b", "L2_gnn_prelu_a",
        "L3_gnn_W_enc", "L3_gnn_b_enc", "L3_gnn_W_rel", "L3_gnn_W_self", "L3_gnn_bias"]


def kernel(**inputs):
    import numpy as _np
    import concourse.bacc as _bacc
    from concourse import mybir as _mybir
    from concourse.bass_utils import run_bass_kernel_spmd as _run

    nc = _bacc.Bacc("TRN2", target_bir_lowering=False, num_devices=1)
    arrays, args = {}, {}
    for name in _INS:
        a = _np.ascontiguousarray(inputs[name])
        arrays[f"in_{name}_dram"] = a
        args[name] = nc.dram_tensor(f"in_{name}_dram", a.shape, _mybir.dt.from_np(a.dtype),
                                    kind="ExternalInput").ap()
    n, d = inputs["x"].shape
    sizes = {"h1": n, "h2": n, "hw": n, "t8": n * 8, "t65a": n * 65, "t65b": n * 65}
    scratch = {name: nc.dram_tensor(f"table_{name}", (r, d), F32, kind="Internal").ap()
               for name, r in sizes.items()}
    out = nc.dram_tensor("out_0_dram", (n, d), _mybir.dt.float32, kind="ExternalOutput").ap()
    bass_gnn(nc, args, out, scratch)
    r = _run(nc, [arrays], core_ids=[0])
    return r.results[0]["out_0_dram"]
```

```python
from contextlib import ExitStack

import concourse.bass as bass
from concourse import mybir

F32 = mybir.dt.float32
BF16 = mybir.dt.bfloat16
I32 = mybir.dt.int32
ALU = mybir.AluOpType
ACT = mybir.ActivationFunctionType
AX = mybir.AxisListType

D = 64
TILE = 16
QUART = TILE // 4
GROUP = 128 * TILE
ACT_TILES = 7
WIN = 200
STEP = 119
SHIFT = 20
BLK = 125
NOWHERE = 10000.0
EPS = 1e-5
PASSES = 7
GIN, RGCN, GCN, REL = (0, 1, 2), (3, 4), 5, 6


def bass_gnn(nc, A, out, scratch):
    N = A["x"].shape[0]
    E = A["src"].shape[0]
    R65 = A["L1_gnn_W"].shape[1]
    R8 = A["L3_gnn_W_rel"].shape[0]
    NG = -(-E // GROUP)
    NB = N // BLK
    SLOTS = -(-(N + SHIFT) // WIN) * WIN
    SWEEPS = SLOTS // WIN
    LAST = E - (NG - 1) * GROUP
    TW = R65 * D
    CHUNKS = [(c, min(512, TW - c)) for c in range(0, TW, 512)]
    PHASES = 5
    XBANKS = -(-NB // 4)
    assert NG % 2 == 0 and NB == NG - 1 and NB * BLK == N and STEP * (NG - 1) + WIN <= SLOTS
    PAIRS = NG // 2

    with ExitStack() as ctx:
        def sb(name, shape, dt=F32):
            return ctx.enter_context(nc.sbuf_tensor(name, shape, dt))

        def pb(name):
            return ctx.enter_context(nc.psum_tensor(name, [128, 512], F32))

        sems = {}

        def sem(*name):
            key = "_".join(str(x) for x in name)
            if key not in sems:
                sems[key] = ctx.enter_context(nc.semaphore("s_" + key))
            return sems[key]

        src_i = sb("src_i", [128, NG * TILE], I32)
        dst_i = sb("dst_i", [128, NG * TILE], I32)
        t65_i = sb("t65_i", [128, NG * TILE], I32)
        t8_i = sb("t8_i", [128, NG * TILE], I32)
        edge_w = sb("edge_w", [128, NG * TILE])
        row_65 = sb("row_65", [128, NG * TILE], I32)
        row_8 = sb("row_8", [128, NG * TILE], I32)
        slot_f = sb("slot_f", [128, NG * TILE])
        t65_bf = sb("t65_bf", [128, NG * TILE], BF16)
        mean_w = sb("mean_w", [128, NG * TILE])
        above_window = sb("above_window", [128, NG * TILE])
        above_block = sb("above_block", [128, NG * TILE])
        last_mask = sb("last_mask", [128, TILE])
        iota_win = sb("iota_win", [128, WIN])
        iota_type = sb("iota_type", [128, TILE * R65], BF16)
        group_base = sb("group_base", [128, NG])
        block_base = sb("block_base", [128, NG])
        sweep_base = sb("sweep_base", [128, SWEEPS])
        ident = sb("ident", [128, 128])
        ident_bf = sb("ident_bf", [128, 128], BF16)
        ident_twice = sb("ident_twice", [D, 2, D])
        ones = sb("ones", [128, 1])
        zeros = sb("zeros", [D, BLK])
        eps = sb("eps", [128, 1])
        worst = sb("worst", [128, 3])
        flag_f = sb("flag_f", [128, 1])
        flag_i = sb("flag_i", [1, 1], I32)
        rows_now = sb("rows_now", [128, 2, TILE], I32)
        msgs = sb("msgs", [128, 2, TILE, D])
        hot = sb("hot", [128, 2, TILE, WIN])
        rel_now = sb("rel_now", [128, 2, TILE])
        w_now = sb("w_now", [128, 2, TILE])
        distance = sb("distance", [128, ACT_TILES, WIN])
        hot_bf = sb("hot_bf", [128, TILE, WIN], BF16)
        type_hot = sb("type_hot", [128, TILE, R65], BF16)
        type_hot_t = sb("type_hot_t", [R65, TILE, 128], BF16)
        inv_now = sb("inv_now", [R65, 3, WIN], BF16)
        inv_rest = sb("inv_rest", [R65, WIN])
        mean_now = sb("mean_now", [128, TILE])
        junk = sb("junk", [128, 4, WIN])
        acc = sb("acc", [D, SLOTS])
        counts = sb("counts", [R65, SLOTS])
        x_fm = sb("x_fm", [D, N])
        h_fm = sb("h_fm", [D, N])
        x_nm = sb("x_nm", [BLK, NB, D])
        hws_nm = sb("hws_nm", [BLK, NB, D])
        dinv = sb("dinv", [BLK, NB])
        in_blk = sb("in_blk", [D, BLK])
        hid_blk = sb("hid_blk", [128, BLK])
        out_blk = sb("out_blk", [D, BLK])
        res_blk = sb("res_blk", [D, BLK])
        y_blk = sb("y_blk", [D, BLK])
        xblk = sb("xblk", [D, BLK])
        x_hi_mid = sb("x_hi_mid", [128, BLK], BF16)
        x_hi_lo = sb("x_hi_lo", [128, BLK], BF16)
        x_rest = sb("x_rest", [128, BLK])
        nm_blk = sb("nm_blk", [BLK, D])
        z_blk = sb("z_blk", [BLK, 2, D])
        y_nm = sb("y_nm", [BLK, D])
        neg_nm = sb("neg_nm", [BLK, D])
        stats = sb("stats", [BLK, 6])
        mean_var = sb("mean_var", [BLK, 2])
        std = sb("std", [BLK, 1])
        rstd = sb("rstd", [BLK, 1])
        table_blk = sb("table_blk", [128, TW])
        w_hi = sb("w_hi", [128, TW], BF16)
        w_mid = sb("w_mid", [128, TW], BF16)
        w_lo_hi = sb("w_lo_hi", [128, TW], BF16)
        w8 = sb("w8", [D, R8 * D])
        gin_w1 = [sb(f"gin_w1_{p}", [D, A[f"L0_gnn_w{p + 1}1"].shape[1]]) for p in GIN]
        gin_w2 = [sb(f"gin_w2_{p}", [A[f"L0_gnn_w{p + 1}2"].shape[0], D]) for p in GIN]
        gin_b1 = [sb(f"gin_b1_{p}", [A[f"L0_gnn_w{p + 1}1"].shape[1], 1]) for p in GIN]
        gin_b2 = [sb(f"gin_b2_{p}", [D, 1]) for p in GIN]
        root = [sb(f"root{n}", [D, D]) for n in range(2)]
        res_w = [sb(f"res_w{n}", [D, D]) for n in range(2)]
        rg_b = [sb(f"rg_b{n}", [D, 1]) for n in range(2)]
        res_b = [sb(f"res_b{n}", [D, 1]) for n in range(2)]
        gcn_w = sb("gcn_w", [D, D])
        gcn_wt = sb("gcn_wt", [D, D])
        gcn_b = sb("gcn_b", [BLK, D])
        prelu_a = sb("prelu_a", [BLK, 1])
        w_enc = sb("w_enc", [D, D])
        b_enc = sb("b_enc", [D, 1])
        w_self = sb("w_self", [D, D])
        rel_b = sb("rel_b", [D, 1])
        sum_ps = [pb("sum_ps0"), pb("sum_ps1")]
        aux_ps = [pb("aux_ps0"), pb("aux_ps1")]
        post_ps = pb("post_ps")
        tab_ps = [pb(f"tab_ps{n}") for n in range(3)]
        fm_a = post_ps[:, 0:BLK]
        fm_b = post_ps[:, 128:128 + BLK]
        nm_ps = post_ps[0:BLK, 256:256 + D]

        def iota_ps(p):
            return (tab_ps[2] if p < 2 else aux_ps[0])[:, 0:WIN]

        gathers = [(A["x"], src_i), (scratch["h1"], src_i), (scratch["h2"], src_i),
                   (scratch["t65a"], row_65), (scratch["t65b"], row_65), (scratch["hw"], src_i),
                   (scratch["t8"], row_8)]
        edge_scale = [edge_w, edge_w, edge_w, mean_w, mean_w, None, None]

        per_step = ("rows_staged", "summed", "hot_done", "added", "type_hot_done", "act_hot_done")
        per_block = {
            "in_done": (range(PASSES), 1), "cleared": (range(6), 1),
            "hidden": (GIN, 1), "hidden_relu": (GIN, 1), "gin_out": (GIN, 1),
            "out_done": ((0, 1, 2, 5), 1), "out_turned": ((0, 1), 1), "rows_ready": ((0, 1, 4, 5, 6), 1),
            "y_done": ((2, 4, 5, 6), 1), "y_turned": ((2, 4, 6), 1), "stats": ((2, 4, 5, 6), 1),
            "moments": ((2, 4, 5, 6), 1), "std_done": ((2, 4, 5, 6), 1), "rstd": ((2, 4, 5, 6), 1),
            "z_done": ((2, 4, 5), 1), "z_turned": ((2, 4, 5), 1), "xblk_done": ((4, 5), 1),
            "parts_begun": ((2, 3), 1), "parts": ((2, 3), 3),
            "conv_mult": ((3, 4, 6), 1), "conv_sum": ((3, 4, 6), 1), "conv_relu": ((3, 4, 6), 1),
            "tab_act": ((2, 3), 5), "tab_dve": ((2, 3), 4)}

        def before(name, p, general):
            steps = SWEEPS * NG if general else NG
            if name in per_step:
                return p * steps
            if name == "distances":
                return 2 * p * steps
            if name == "staged":
                return sum(steps * (1 if edge_scale[q] is None else 2) for q in range(p))
            if name == "gathered":
                return p // 2 * steps // 2 * 16 * QUART
            if name == "tab_mult":
                return NB * sum({2: 9, 3: 9, 5: 1}.get(q, 0) for q in range(p))
            if name == "stored":
                return 16 + NB * sum(32 if q in (2, 3) else 16 for q in range(p))
            users, n = per_block[name]
            return (name == "cleared") + NB * n * sum(q < p for q in users)

        def load_edges(eng, tile, src, done):
            full = (NG - 1) * GROUP
            t = tile[:, :].rearrange("p (g j) -> p g j", j=TILE)
            eng.dma_start(t[:, 0:NG - 1, :], src[0:full].rearrange("(g p j) -> p g j", p=128, j=TILE))\
               .then_inc(sem(done), 16)
            rows, rest = LAST // TILE, LAST % TILE
            eng.dma_start(t[0:rows, NG - 1, :],
                          src[full:full + rows * TILE].rearrange("(p j) -> p j", j=TILE))\
               .then_inc(sem(done), 16)
            eng.dma_start(t[rows:rows + 1, NG - 1, 0:rest],
                          src[full + rows * TILE:E].rearrange("(a j) -> a j", a=1))\
               .then_inc(sem(done), 16)

        small = [(gcn_w, A["L2_gnn_W"]), (w_enc, A["L3_gnn_W_enc"]), (w_self, A["L3_gnn_W_self"])]
        cols = [(b_enc, A["L3_gnn_b_enc"]), (rel_b, A["L3_gnn_bias"])]
        for p in GIN:
            small += [(gin_w1[p], A[f"L0_gnn_w{p + 1}1"]), (gin_w2[p], A[f"L0_gnn_w{p + 1}2"])]
            cols += [(gin_b1[p], A[f"L0_gnn_b{p + 1}1"]), (gin_b2[p], A[f"L0_gnn_b{p + 1}2"])]
        for n in range(2):
            small += [(root[n], A["L1_gnn_root"][n]), (res_w[n], A["L1_gnn_res_W"][n])]
            cols += [(rg_b[n], A["L1_gnn_bias"][n]), (res_b[n], A["L1_gnn_res_b"][n])]
        WEIGHTS = 16 * (len(small) + len(cols) + 2 + 1)

        def at(tile, n, w=1):
            return tile[:, n:n + w] if isinstance(n, int) else tile[:, bass.ds(n, w)]

        def cols_of(tile, b):
            return at(tile, b * BLK, BLK)

        def sums_of(b):
            return at(acc, b * BLK + SHIFT, BLK)

        def col16(tile, g):
            return at(tile, g * TILE, TILE)

        def nm_at(tile, b):
            return tile[:, b, :] if isinstance(b, int) else \
                tile[:, bass.ds(b, 1), :].rearrange("p a d -> p (a d)")

        def schedule(eng, general, turn, finish, setup=None):
            if general:
                with eng.Fori(0, SWEEPS) as k:
                    with eng.Fori(0, PAIRS) as i:
                        for u in range(2):
                            turn(k * NG + 2 * i + u, 2 * i + u, k, u, k * PAIRS + i, None)
                if setup:
                    setup()
                with eng.Fori(0, NB) as b:
                    for i in range(PHASES):
                        finish(i, b)
                return
            turn(0, 0, None, 0, 0, None)
            turn(1, 1, None, 1, 0, None)
            if setup:
                setup()
            with eng.Fori(1, PAIRS - 1) as i:
                for u in range(2):
                    s = 2 * i + u
                    turn(s, s, None, u, i, s - 2)
            turn(NG - 2, NG - 2, None, 0, PAIRS - 1, NG - 4)
            turn(NG - 1, NG - 1, None, 1, PAIRS - 1, NG - 3)

        def finish_last(p, finish, table):
            for i in range(PHASES):
                finish(i, NB - 1)
                if p in (2, 3) and i < 3:
                    table(NB - 2, range(3 * i, 3 * i + 3))

        def phases_in_turn(p, s):
            return PHASES - 1 if p in (2, 3) and isinstance(s, int) and s == NG - 1 else PHASES

        def looks_in_turn(p, general, s):
            return p == 1 and (general or not (isinstance(s, int) and s == NG - 1))

        def ahead(p, s):
            return (p + 1, 0) if isinstance(s, int) and s == NG - 1 else (p, s + 1)

        def by_branch(eng, run):
            eng.wait_ge(sem("flag_ready"), 1)
            general = eng.value_load(flag_i[0:1, 0:1], min_val=0, max_val=1)
            with eng.If(general == 0):
                run(False)
            with eng.Else():
                run(True)

        block = ctx.enter_context(nc.Block())

        @block.sync
        def _(sp):
            sp.wait_ge(sem("pads_set"), 5)
            load_edges(sp, dst_i, A["dst"], "dst_in")
            load_edges(sp, src_i, A["src"], "src_in")
            for tile, name in ((edge_w, "edge_weight"), (t65_i, "edge_type_65"), (t8_i, "edge_type_8")):
                load_edges(sp, tile, A[name], "edges_in")
            sp.dma_start(x_nm[:, :, :], A["x"].rearrange("(b p) d -> p b d", p=BLK))\
              .then_inc(sem("x_in"), 16)
            for tile, w in small:
                sp.dma_start(tile[:, :], w).then_inc(sem("weights_in"), 16)
            for tile, w in cols:
                sp.dma_start(tile[:, :], w.rearrange("(d a) -> d a", a=1)).then_inc(sem("weights_in"), 16)
            sp.dma_start(gcn_b[:, :], A["L2_gnn_b"].rearrange("(a d) -> a d", a=1).to_broadcast([BLK, D]))\
              .then_inc(sem("weights_in"), 16)
            sp.dma_start(prelu_a[:, :], A["L2_gnn_prelu_a"].rearrange("(a d) -> a d", a=1)
                         .to_broadcast([BLK, 1])).then_inc(sem("weights_in"), 16)
            sp.dma_start(w8[:, :].rearrange("d (r k) -> d r k", k=D),
                         A["L3_gnn_W_rel"].rearrange("r d k -> d r k")).then_inc(sem("weights_in"), 16)

            def load_w65(n):
                for half in range(2):
                    sp.dma_start(table_blk[half * D:(half + 1) * D, :].rearrange("d (r k) -> d r k", k=D),
                                 A["L1_gnn_W"][n].rearrange("r d k -> d r k")).then_inc(sem("w65_in"), 16)

            load_w65(0)
            sp.sem_inc(sem("stored"), 16)
            node_tables = {0: scratch["h1"], 1: scratch["h2"], 4: scratch["hw"], 6: out}
            wide_tables = {2: scratch["t65a"].rearrange("(n t) d -> n (t d)", t=R65),
                           3: scratch["t65b"].rearrange("(n t) d -> n (t d)", t=R65),
                           5: scratch["t8"].rearrange("(n t) d -> n (t d)", t=R8)}

            def rows(table, b):
                return table[b * BLK:(b + 1) * BLK, :] if isinstance(b, int) else \
                    table[bass.ds(b * BLK, BLK), :]

            def run(general):
                for p in range(PASSES):
                    if p == 3:
                        sp.wait_ge(sem("stored"), before("stored", p, general))
                        load_w65(1)
                    with sp.Fori(0, NB) as b:
                        if p in (2, 3):
                            for part, (o, end) in enumerate(((0, CHUNKS[4][0]), (CHUNKS[4][0], TW))):
                                sp.wait_ge(sem("tab_act"), before("tab_act", p, general) + 5 * b + 2 + 3 * part)
                                sp.sem_inc(sem("sp_turns"), 1)
                                sp.wait_ge(sem("tab_dve"), before("tab_dve", p, general) + 4 * b + 2 + 2 * part)
                                sp.sem_inc(sem("sp_turns"), 1)
                                sp.dma_start(rows(wide_tables[p], b)[:, o:end], table_blk[0:BLK, o:end])\
                                  .then_inc(sem("stored"), 16)
                        else:
                            sp.wait_ge(sem("rows_ready"), before("rows_ready", p, general) + b + 1)
                            if p == 5:
                                sp.dma_start(rows(wide_tables[p], b), table_blk[0:BLK, 0:R8 * D])\
                                  .then_inc(sem("stored"), 16)
                            else:
                                sp.dma_start(rows(node_tables[p], b),
                                             z_blk[:, 0, :] if p == REL else nm_blk[:, :])\
                                  .then_inc(sem("stored"), 16)
                sp.wait_ge(sem("stored"), before("stored", PASSES, general))

            by_branch(sp, run)

        @block.gpsimd
        def _(pool):
            last = slice((NG - 1) * TILE, NG * TILE)
            pool.memset(dst_i[:, last], N - 1).then_inc(sem("pads_set"), 1)
            pool.memset(src_i[:, last], 0).then_inc(sem("pads_set"), 1)
            pool.memset(t65_i[:, last], 0).then_inc(sem("pads_set"), 1)
            pool.memset(t8_i[:, last], 0).then_inc(sem("pads_set"), 1)
            pool.memset(edge_w[:, last], 0.0).then_inc(sem("pads_set"), 1)
            pool.memset(ones[:, :], 1.0).then_inc(sem("consts"), 1)
            pool.iota(group_base[:, :], pattern=[[STEP, NG]], base=0, channel_multiplier=0,
                      allow_small_or_imprecise_dtypes=True).then_inc(sem("consts"), 1)
            pool.iota(block_base[:, :], pattern=[[BLK, NG]], base=SHIFT - BLK, channel_multiplier=0,
                      allow_small_or_imprecise_dtypes=True).then_inc(sem("consts"), 1)
            pool.iota(sweep_base[:, :], pattern=[[WIN, SWEEPS]], base=0, channel_multiplier=0,
                      allow_small_or_imprecise_dtypes=True).then_inc(sem("consts"), 1)
            pool.iota(iota_win[:, :], pattern=[[1, WIN]], base=0, channel_multiplier=0,
                      allow_small_or_imprecise_dtypes=True).then_inc(sem("consts"), 1)
            pool.memset(last_mask[:, :], 1.0).then_inc(sem("masks_begun"), 1)
            pool.memset(ident[:, :], 0.0).then_inc(sem("masks_begun"), 1)
            pool.wait_ge(sem("masks_begun"), 2)
            pool.affine_select(out=last_mask[:, :], in_=last_mask[:, :], compare_op=ALU.is_ge, fill=0.0,
                               base=LAST - 1, pattern=[[-1, TILE]], channel_multiplier=-TILE)\
                .then_inc(sem("consts"), 1)
            pool.affine_select(out=ident[:, :], in_=ident[:, :], compare_op=ALU.not_equal, fill=1.0,
                               base=0, pattern=[[-1, 128]], channel_multiplier=1).then_inc(sem("consts"), 1)
            pool.iota(iota_type[:, :], pattern=[[0, TILE], [1, R65]], base=0, channel_multiplier=0,
                      allow_small_or_imprecise_dtypes=True).then_inc(sem("consts"), 1)

            def run(general):
                for p in range(PASSES):
                    table = gathers[p][0]
                    if p > 0:
                        pool.wait_ge(sem("stored"), before("stored", p, general))

                    def turn(s, g, k, u, n, b):
                        pool.wait_ge(sem("rows_staged"), before("rows_staged", p, general) + s + 1)
                        pool.sem_inc(sem("pool_turns"), 1)
                        for j in range(TILE):
                            pool.indirect_dma_start(
                                out=msgs[:, u, j, :], out_offset=None, in_=table[:, :],
                                in_offset=bass.IndirectOffsetOnAxis(ap=rows_now[:, u, j:j + 1], axis=0))\
                                .then_inc(sem("gathered", p % 2, u, j // QUART), 16)

                    schedule(pool, general, turn, lambda i, b: None)
                pool.wait_ge(sem("stored"), before("stored", PASSES, general))

            by_branch(pool, run)

        @block.scalar
        def _(act):
            act.wait_ge(sem("edges_in"), 9 * 16)
            act.activation(t65_bf[:, :], t65_i[:, :], ACT.Copy).then_inc(sem("types_cast"), 1)
            act.sem_inc(sem("act_hot_done"), 1)
            act.wait_ge(sem("src_in"), 48)

            def run(general):
                def stage_rows(p, s, g, u):
                    act.wait_ge(sem("summed"), before("summed", p, general) + s + 1)
                    act.sem_inc(sem("act_turns"), 1)
                    act.activation(rows_now[:, u, :], col16(gathers[p][1], g), ACT.Copy)\
                       .then_inc(sem("rows_staged"), 1)

                def one_hots(q, t, u):
                    act.wait_ge(sem("act_hot_done"), before("act_hot_done", q, general) + t + 1)
                    act.sem_inc(sem("act_turns"), 1)
                    act.wait_ge(sem("staged"), before("staged", q, general) + 2 * (t + 1))
                    for n in range(ACT_TILES):
                        j = TILE - ACT_TILES + n
                        last = act.activation(distance[:, n, :], iota_win[:, :], ACT.Abs, scale=-1.0,
                                              bias=rel_now[:, u, j:j + 1])
                    last.then_inc(sem("distances"), 1)
                    act.wait_ge(sem("distances"), before("distances", q, general) + 2 * t + 1)
                    act.activation(distance[:, :, :], distance[:, :, :], ACT.Relu, scale=-1.0,
                                   bias=ones[:, :]).then_inc(sem("distances"), 1)
                    act.wait_ge(sem("distances"), before("distances", q, general) + 2 * t + 2)
                    for n in range(ACT_TILES):
                        j = TILE - ACT_TILES + n
                        last = act.activation(hot[:, u, j, :], distance[:, n, :], ACT.Copy,
                                              scale=w_now[:, u, j:j + 1])
                    last.then_inc(sem("act_hot_done"), 1)

                if not general:
                    stage_rows(0, 0, 0, 0)
                    one_hots(0, 0, 0)
                for p in range(PASSES):
                    def turn(s, g, k, u, n, b):
                        if general:
                            stage_rows(p, s, g, u)
                            if p < 2:
                                one_hots(p, s, u)
                        elif ahead(p, s)[0] < PASSES:
                            q, t = ahead(p, s)
                            stage_rows(q, t, t, 1 - u)
                        if b is not None:
                            finish(0, b)
                            finish(1, b)
                        if looks_in_turn(p, general, s):
                            take_types(s)
                        if not general and ahead(p, s)[0] < 2:
                            one_hots(*ahead(p, s), 1 - u)
                        if b is not None:
                            for i in range(2, phases_in_turn(p, s)):
                                finish(i, b)

                    def take_types(s):
                        act.wait_ge(sem("summed"), before("summed", p, general) + s + 2)
                        for h in range(2):
                            act.wait_ge(sem("type_turned"), 2 * s + h + 1)
                            act.sem_inc(sem("act_turns"), 1)
                            act.activation(type_hot_t[:, 8 * h:8 * h + 8, :].rearrange("t j e -> t (j e)"),
                                           aux_ps[h][0:R65, :].bitcast(BF16), ACT.Copy)\
                               .then_inc(sem("type_hot_t_done"), 1)

                    def root_of_variance(b):
                        act.wait_ge(sem("moments"), before("moments", p, general) + b + 1)
                        act.activation(std[:, :], mean_var[:, 1:2], ACT.Sqrt, bias=eps[0:BLK, :])\
                           .then_inc(sem("std_done"), 1)

                    def back(b):
                        act.wait_ge(sem("z_turned"), before("z_turned", p, general) + b + 1)
                        act.sem_inc(sem("act_turns"), 1)
                        act.activation(cols_of(x_fm, b), fm_a[0:D, :], ACT.Copy)
                        act.activation(xblk[:, :], fm_a[0:D, :], ACT.Copy).then_inc(sem("xblk_done"), 1)

                    def high_parts(b):
                        if p == 2:
                            act.wait_ge(sem("z_turned"), before("z_turned", p, general) + b + 1)
                            act.sem_inc(sem("act_turns"), 1)
                            act.activation(cols_of(x_fm, b), fm_a[0:D, :], ACT.Copy)
                        else:
                            act.wait_ge(sem("h_doubled"), b + 1)
                        act.activation(x_hi_mid[:, :], fm_a, ACT.Copy)
                        act.activation(x_hi_lo[:, :], fm_a, ACT.Copy).then_inc(sem("parts_begun"), 1)

                    def table(b, chunks):
                        if 0 in chunks:
                            act.wait_ge(sem("stored"), before("stored", p, general) + 32 * b)
                        for c in chunks:
                            if c % 2:
                                continue
                            o, w = CHUNKS[c]
                            act.wait_ge(sem("tab_mult"), before("tab_mult", p, general) + 9 * b + c + 1)
                            act.activation(table_blk[0:BLK, o:o + w], tab_ps[c % 3][0:BLK, 0:w], ACT.Copy)\
                               .then_inc(sem("tab_act"), 1)

                    def finish(i, b):
                        if p in GIN:
                            if i == 0:
                                f = gin_w1[p].shape[1]
                                act.wait_ge(sem("hidden"), before("hidden", p, general) + b + 1)
                                act.activation(hid_blk[0:f, :], fm_a[0:f, :], ACT.Relu, bias=gin_b1[p][:, :])\
                                   .then_inc(sem("hidden_relu"), 1)
                            elif i == 1:
                                act.wait_ge(sem("gin_out"), before("gin_out", p, general) + b + 1)
                                act.sem_inc(sem("act_turns"), 1)
                                if p < 2:
                                    act.activation(cols_of(h_fm, b), fm_b[0:D, :], ACT.Relu,
                                                   bias=gin_b2[p][:, :])
                                act.activation(out_blk[:, :], fm_b[0:D, :], ACT.Relu if p < 2 else ACT.Identity,
                                               bias=gin_b2[p][:, :]).then_inc(sem("out_done"), 1)
                            elif p == 2 and i == 2:
                                root_of_variance(b)
                            elif p == 2 and i == 3:
                                high_parts(b)
                            elif p == 2:
                                table(b, range(len(CHUNKS)))
                        elif p in RGCN:
                            if i == 0:
                                act.wait_ge(sem("conv_sum"), before("conv_sum", p, general) + b + 1)
                                act.activation(out_blk[:, :], y_blk[:, :], ACT.Relu, bias=rg_b[p - 3][:, :])
                                act.activation(res_blk[:, :], fm_b[0:D, :], ACT.Relu, bias=res_b[p - 3][:, :])\
                                   .then_inc(sem("conv_relu"), 1)
                            elif p == 3 and i == 3:
                                high_parts(b)
                            elif p == 3 and i == 4:
                                table(b, range(len(CHUNKS)))
                            elif p == 4 and i == 2:
                                root_of_variance(b)
                            elif p == 4 and i == 3:
                                back(b)
                        elif p == GCN:
                            if i == 0:
                                root_of_variance(b)
                            elif i == 1:
                                back(b)
                            elif i == 2:
                                act.wait_ge(sem("encoded"), b + 1)
                                act.sem_inc(sem("act_turns"), 1)
                                act.activation(cols_of(h_fm, b), fm_b[0:D, :], ACT.Relu, bias=b_enc[:, :])
                                act.activation(out_blk[:, :], fm_b[0:D, :], ACT.Relu, bias=b_enc[:, :])\
                                   .then_inc(sem("out_done"), 1)
                            elif i == 3:
                                act.wait_ge(sem("stored"), before("stored", p, general) + 16 * b)
                                act.wait_ge(sem("tab_mult"), before("tab_mult", p, general) + b + 1)
                                act.activation(table_blk[0:BLK, 0:R8 * D], tab_ps[0][0:BLK, 0:R8 * D],
                                               ACT.Copy).then_inc(sem("rows_ready"), 1)
                        else:
                            if i == 0:
                                act.wait_ge(sem("conv_sum"), before("conv_sum", p, general) + b + 1)
                                act.activation(out_blk[:, :], y_blk[:, :], ACT.Relu, bias=rel_b[:, :])\
                                   .then_inc(sem("conv_relu"), 1)
                            elif i == 2:
                                root_of_variance(b)

                    def turn_x():
                        for n in range(XBANKS):
                            w = min(4, NB - 4 * n) * BLK
                            act.wait_ge(sem("x_turned"), n + 1)
                            act.activation(x_fm[:, 4 * n * BLK:4 * n * BLK + w], tab_ps[n % 2][0:D, 0:w],
                                           ACT.Copy).then_inc(sem("x_fm_done"), 1)
                        act.wait_ge(sem("gcn_w_turned"), 1)
                        act.activation(gcn_wt[:, :], post_ps[0:D, 0:D], ACT.Copy)\
                           .then_inc(sem("gcn_wt_done"), 1)

                    def split_w():
                        layer = p - 2
                        act.wait_ge(sem("w65_in"), 32 * (layer + 1))
                        if p == 3:
                            act.wait_ge(sem("tab_mult"), before("tab_mult", p, general))
                        act.activation(w_hi[:, :], table_blk[:, :], ACT.Copy).then_inc(sem("w_high"), 1)
                        act.wait_ge(sem("w_high"), layer + 1)
                        act.activation(w_lo_hi[D:128, :], w_hi[D:128, :], ACT.Copy).then_inc(sem("w_high_again"), 1)
                        act.wait_ge(sem("w_rest"), layer + 1)
                        act.activation(w_mid[:, :], table_blk[:, :], ACT.Copy).then_inc(sem("w_middle"), 1)

                    schedule(act, general, turn, finish, {0: turn_x, 2: split_w, 3: split_w}.get(p))
                    if not general:
                        finish_last(p, finish, table)
                        if p == 1:
                            take_types(NG - 1)
                    if p == 0:
                        act.wait_ge(sem("degrees"), 1)
                        act.activation(dinv[:, :], aux_ps[0][0:BLK, 0:NB], ACT.Sqrt, bias=ones[0:BLK, :])\
                           .then_inc(sem("degree_root"), 1)

            by_branch(act, run)

        @block.tensor
        def _(pe):
            pe.wait_ge(sem("consts"), 8)
            pe.sem_inc(sem("summed"), 2)
            pe.wait_ge(sem("outside_done"), 1)
            pe.matmul(post_ps[0:1, 0:1], flag_f[:, :], ones[:, :]).then_inc(sem("outside_sum"), 1)

            def run(general):
                for p in range(PASSES):
                    def count(s, u):
                        pe.wait_ge(sem("type_hot_done"), s + 1)
                        for j in range(TILE):
                            pe.matmul(aux_ps[u][0:R65, 0:WIN], type_hot[:, j, :], hot_bf[:, j, :],
                                      start=(j == 0), stop=(j == TILE - 1))

                    def turn_types(s):
                        pe.wait_ge(sem("type_hot_done"), before("type_hot_done", p, general) + s + 1)
                        pe.sem_inc(sem("pe_turns"), 1)
                        for j in range(TILE):
                            bank = aux_ps[j // 8][0:R65, :].bitcast(BF16)
                            last = pe.transpose(bank[:, (j % 8) * 128:(j % 8 + 1) * 128],
                                                type_hot[:, j, :], ident_bf[:, :])
                            if j % 8 == 7:
                                last.then_inc(sem("type_turned"), 1)

                    def look_up(i, s):
                        for j in range(QUART * i, QUART * (i + 1)):
                            if j == 0:
                                pe.wait_ge(sem("inv_parts"), 4 * s + 4)
                            if j % 8 == 0:
                                pe.wait_ge(sem("type_hot_t_done"), 2 * s + j // 8 + 1)
                            if j % 2 == 0:
                                pe.wait_ge(sem("look_used"), TILE // 2 * s + j // 2 + 1)
                                pe.sem_inc(sem("pe_turns"), 1)
                            for part in range(3):
                                last = pe.matmul(tab_ps[j // 2 % 2][:, (j % 2) * WIN:(j % 2 + 1) * WIN],
                                                 type_hot_t[:, j, :], inv_now[:, part, :],
                                                 start=(part == 0), stop=(part == 2))
                            if j % 2:
                                last.then_inc(sem("look_done"), 1)

                    def sum_up(i, s, u, n):
                        if i == 0 and p < 2:
                            pe.wait_ge(sem("act_hot_done"), before("act_hot_done", p, general) + s + 2)
                            pe.sem_inc(sem("pe_turns"), 1)
                        if i == 0:
                            pe.wait_ge(sem("hot_done"), before("hot_done", p, general) + s + 1)
                        pe.wait_ge(sem("gathered", p % 2, u, i),
                                   before("gathered", p, general) + 16 * QUART * (n + 1))
                        for j in range(QUART * i, QUART * (i + 1)):
                            last = pe.matmul(sum_ps[u][0:D, 0:WIN], msgs[:, u, j, :], hot[:, u, j, :],
                                             start=(j == 0), stop=(j == TILE - 1))
                        if i == 3:
                            last.then_inc(sem("summed"), 1)

                    def turn(s, g, k, u, n, b):
                        if b is not None:
                            finish(0, b)
                        for i in range(4):
                            if p == 0 and i == 1:
                                count(s, u)
                            sum_up(i, s, u, n)
                            if b is not None and i + 1 < phases_in_turn(p, s):
                                finish(i + 1, b)
                            if looks_in_turn(p, general, s):
                                if i == 0:
                                    turn_types(s)
                                look_up(i, s)

                    def turn_y(b):
                        pe.wait_ge(sem("y_done"), before("y_done", p, general) + b + 1)
                        pe.sem_inc(sem("pe_turns"), 1)
                        pe.transpose(nm_ps, y_blk[:, :], ident[0:D, 0:D]).then_inc(sem("y_turned"), 1)

                    def turn_z(b):
                        pe.wait_ge(sem("z_done"), before("z_done", p, general) + b + 1)
                        pe.sem_inc(sem("pe_turns"), 1)
                        if p == 2:
                            pe.transpose(fm_a, z_blk[:, :, :].rearrange("n a d -> n (a d)"),
                                         ident[0:BLK, 0:BLK]).then_inc(sem("z_turned"), 1)
                        else:
                            pe.transpose(fm_a[0:D, :], z_blk[:, 0, :], ident[0:BLK, 0:BLK])\
                              .then_inc(sem("z_turned"), 1)

                    def table(b, chunks):
                        if 0 in chunks:
                            pe.wait_ge(sem("parts"), before("parts", p, general) + 3 * b + 3)
                            pe.sem_inc(sem("pe_turns"), 1)
                        for c in chunks:
                            o, w = CHUNKS[c]
                            if c >= 3:
                                if c % 2:
                                    pe.wait_ge(sem("tab_act"), before("tab_act", p, general)
                                               + 5 * b + (c - 3) // 2 + 1)
                                else:
                                    pe.wait_ge(sem("tab_dve"), before("tab_dve", p, general)
                                               + 4 * b + (c - 3) // 2 + 1)
                                pe.sem_inc(sem("pe_turns"), 1)
                            products = ((x_hi_mid, w_hi), (x_hi_mid, w_mid), (x_hi_lo, w_lo_hi))
                            for n, (x_part, w_part) in enumerate(products):
                                last = pe.matmul(tab_ps[c % 3][0:BLK, 0:w], x_part[:, :], w_part[:, o:o + w],
                                                 start=(n == 0), stop=(n == 2))
                            last.then_inc(sem("tab_mult"), 1)

                    def finish(i, b):
                        if p in GIN:
                            f = gin_w1[p].shape[1]
                            if i == 0:
                                pe.wait_ge(sem("in_done"), before("in_done", p, general) + b + 1)
                                pe.sem_inc(sem("pe_turns"), 1)
                                pe.matmul(fm_a[0:f, :], gin_w1[p][:, :], in_blk[:, :]).then_inc(sem("hidden"), 1)
                            elif i == 1:
                                pe.wait_ge(sem("hidden_relu"), before("hidden_relu", p, general) + b + 1)
                                pe.sem_inc(sem("pe_turns"), 1)
                                pe.matmul(fm_b[0:D, :], gin_w2[p][:, :], hid_blk[0:f, :])\
                                  .then_inc(sem("gin_out"), 1)
                            elif p < 2 and i == 2:
                                pe.wait_ge(sem("out_done"), before("out_done", p, general) + b + 1)
                                pe.sem_inc(sem("pe_turns"), 1)
                                pe.transpose(nm_ps, out_blk[:, :], ident[0:D, 0:D])\
                                  .then_inc(sem("out_turned"), 1)
                            elif p == 2 and i == 2:
                                turn_y(b)
                            elif p == 2 and i == 3:
                                turn_z(b)
                            elif p == 2:
                                table(b, range(len(CHUNKS)))
                        elif p in RGCN:
                            if i == 0:
                                pe.wait_ge(sem("in_done"), before("in_done", p, general) + b + 1)
                                pe.sem_inc(sem("pe_turns"), 1)
                                pe.matmul(fm_a[0:D, :], root[p - 3][:, :], in_blk[:, :])
                                pe.matmul(fm_b[0:D, :], res_w[p - 3][:, :], in_blk[:, :])\
                                  .then_inc(sem("conv_mult"), 1)
                            elif p == 3 and i == 3:
                                pe.wait_ge(sem("h_done"), b + 1)
                                pe.sem_inc(sem("pe_turns"), 1)
                                pe.matmul(fm_a, ident_twice[:, :, :].rearrange("d a k -> d (a k)"), xblk[:, :])\
                                  .then_inc(sem("h_doubled"), 1)
                            elif p == 3 and i == 4:
                                table(b, range(len(CHUNKS)))
                            elif p == 4 and i == 2:
                                turn_y(b)
                            elif p == 4 and i == 3:
                                turn_z(b)
                            elif p == 4 and i == 4:
                                pe.wait_ge(sem("xblk_done"), before("xblk_done", p, general) + b + 1)
                                pe.sem_inc(sem("pe_turns"), 1)
                                pe.matmul(nm_ps, xblk[:, :], gcn_wt[:, :]).then_inc(sem("gcn_mult"), 1)
                        elif p == GCN:
                            if i == 0:
                                pe.wait_ge(sem("in_done"), before("in_done", p, general) + b + 1)
                                pe.sem_inc(sem("pe_turns"), 1)
                                pe.transpose(nm_ps, in_blk[:, :], ident[0:D, 0:D])\
                                  .then_inc(sem("sum_turned"), 1)
                            elif i == 1:
                                turn_z(b)
                            elif i == 2:
                                pe.wait_ge(sem("xblk_done"), before("xblk_done", p, general) + b + 1)
                                pe.sem_inc(sem("pe_turns"), 1)
                                pe.matmul(fm_b[0:D, :], w_enc[:, :], xblk[:, :]).then_inc(sem("encoded"), 1)
                            elif i == 3:
                                pe.wait_ge(sem("out_done"), before("out_done", p, general) + b + 1)
                                pe.sem_inc(sem("pe_turns"), 1)
                                pe.matmul(tab_ps[0][0:BLK, 0:R8 * D], out_blk[:, :], w8[:, :])\
                                  .then_inc(sem("tab_mult"), 1)
                        else:
                            if i == 0:
                                pe.wait_ge(sem("in_done"), before("in_done", p, general) + b + 1)
                                pe.sem_inc(sem("pe_turns"), 1)
                                pe.matmul(fm_a[0:D, :], w_self[:, :], in_blk[:, :]).then_inc(sem("conv_mult"), 1)
                            elif i == 1:
                                turn_y(b)

                    def wait_for_w():
                        pe.wait_ge(sem("w_split"), p - 1)

                    def turn_x():
                        pe.wait_ge(sem("x_in"), 16)
                        for n in range(XBANKS):
                            if n >= 2:
                                pe.wait_ge(sem("x_fm_done"), n - 1)
                            for b in range(4 * n, min(4 * n + 4, NB)):
                                o = (b % 4) * BLK
                                last = pe.transpose(tab_ps[n % 2][0:D, o:o + BLK], x_nm[:, b, :],
                                                    ident[0:BLK, 0:BLK])
                            last.then_inc(sem("x_turned"), 1)
                        pe.wait_ge(sem("weights_in"), WEIGHTS)
                        pe.transpose(post_ps[0:D, 0:D], gcn_w[:, :], ident[0:D, 0:D])\
                          .then_inc(sem("gcn_w_turned"), 1)
                        pe.wait_ge(sem("gcn_wt_done"), 1)

                    schedule(pe, general, turn, finish,
                             {0: turn_x, 2: wait_for_w, 3: wait_for_w}.get(p))
                    if not general:
                        finish_last(p, finish, table)
                        if p == 1:
                            turn_types(NG - 1)
                            for i in range(4):
                                look_up(i, NG - 1)
                    if p == 0:
                        pe.wait_ge(sem("counts_done"), SWEEPS * NG if general else NG)
                        for b in range(NB):
                            o = SHIFT + b * BLK
                            last = pe.matmul(aux_ps[0][0:BLK, b:b + 1], counts[:, o:o + BLK], ones[0:R65, :])
                        last.then_inc(sem("degrees"), 1)

            by_branch(pe, run)

        @block.vector
        def _(dve):
            dve.wait_ge(sem("consts"), 8)
            dve.wait_ge(sem("dst_in"), 48)
            dve.tensor_scalar(slot_f[:, :], dst_i[:, :], float(SHIFT), None, ALU.add).then_inc(sem("prep"), 1)
            dve.wait_ge(sem("prep"), 1)
            for above, base in ((above_window, group_base), (above_block, block_base)):
                dve.tensor_tensor(above[:, :].rearrange("p (g j) -> p g j", j=TILE),
                                  slot_f[:, :].rearrange("p (g j) -> p g j", j=TILE),
                                  base[:, :].unsqueeze(2).to_broadcast([128, NG, TILE]), ALU.subtract)\
                   .then_inc(sem("prep"), 1)
            dve.wait_ge(sem("prep"), 3)
            dve.tensor_reduce(worst[:, 0:1], above_window[:, :], AX.X, ALU.max).then_inc(sem("prep"), 1)
            dve.tensor_reduce(worst[:, 1:2], above_window[:, :], AX.X, ALU.min).then_inc(sem("prep"), 1)
            dve.tensor_reduce(worst[:, 2:3], above_block[:, :], AX.X, ALU.min).then_inc(sem("prep"), 1)
            dve.wait_ge(sem("prep"), 6)
            dve.tensor_scalar(worst[:, 0:1], worst[:, 0:1], float(WIN - 1), None, ALU.is_gt)\
               .then_inc(sem("prep"), 1)
            dve.tensor_scalar(worst[:, 1:3], worst[:, 1:3], 0.0, None, ALU.is_lt).then_inc(sem("prep"), 1)
            dve.wait_ge(sem("prep"), 8)
            dve.tensor_reduce(flag_f[:, :], worst[:, :], AX.X, ALU.max).then_inc(sem("outside_done"), 1)
            lastg = slot_f[:, (NG - 1) * TILE:NG * TILE]
            dve.scalar_tensor_tensor(out=lastg, in0=lastg, scalar=NOWHERE, in1=last_mask[:, :],
                                     op0=ALU.add, op1=ALU.mult).then_inc(sem("prep"), 1)
            dve.wait_ge(sem("prep"), 9)
            dve.tensor_scalar(lastg, lastg, -NOWHERE, None, ALU.add).then_inc(sem("prep"), 1)
            dve.wait_ge(sem("outside_sum"), 1)
            dve.tensor_scalar(flag_i[:, :], post_ps[0:1, 0:1], 0.5, None, ALU.is_gt)\
               .then_inc(sem("flag_ready"), 1)
            dve.tensor_copy(iota_ps(0), iota_win[:, :]).then_inc(sem("fills"), 1)
            dve.memset(acc[:, :], 0.0).then_inc(sem("cleared"), 1)
            dve.memset(counts[:, :], 0.0).then_inc(sem("fills"), 1)
            dve.memset(mean_w[:, :], 0.0).then_inc(sem("fills"), 1)
            dve.memset(zeros[:, :], 0.0).then_inc(sem("fills"), 1)
            dve.memset(eps[:, :], EPS).then_inc(sem("fills"), 1)
            dve.tensor_copy(ident_bf[:, :], ident[:, :]).then_inc(sem("prep"), 1)
            dve.tensor_copy(ident_twice[:, :, :], ident[0:D, 0:D].unsqueeze(1).to_broadcast([D, 2, D]))\
               .then_inc(sem("prep"), 1)
            dve.wait_ge(sem("src_in"), 48)
            dve.wait_ge(sem("edges_in"), 9 * 16)
            dve.scalar_tensor_tensor(out=row_65[:, :], in0=src_i[:, :], scalar=float(R65),
                                     in1=t65_i[:, :], op0=ALU.mult, op1=ALU.add).then_inc(sem("prep"), 1)
            dve.scalar_tensor_tensor(out=row_8[:, :], in0=src_i[:, :], scalar=float(R8),
                                     in1=t8_i[:, :], op0=ALU.mult, op1=ALU.add).then_inc(sem("prep"), 1)
            dve.wait_ge(sem("prep"), 14)
            dve.wait_ge(sem("types_cast"), 1)
            dve.wait_ge(sem("fills"), 5)
            dve.sem_inc(sem("look_used"), 2)

            def run(general):
                def stage_edges(p, s, g, k, u):
                    scale = edge_scale[p]
                    dve.wait_ge(sem("summed"), before("summed", p, general) + s + 1)
                    base = at(sweep_base, k) if general else at(group_base, g)
                    dve.tensor_scalar(rel_now[:, u, :], col16(slot_f, g), base, None, ALU.subtract)\
                       .then_inc(sem("staged"), 1)
                    if scale is not None:
                        dve.tensor_copy(w_now[:, u, :], col16(scale, g)).then_inc(sem("staged"), 1)
                    dve.wait_ge(sem("staged"), before("staged", p, general)
                                + (s + 1) * (1 if scale is None else 2))

                def one_hots(i, p, u, columns):
                    mine = TILE - ACT_TILES if p < 2 else TILE
                    for j in range(QUART * i, min(QUART * (i + 1), mine)):
                        if edge_scale[p] is None:
                            last = dve.tensor_scalar(hot[:, u, j, :], columns,
                                                     rel_now[:, u, j:j + 1], None, ALU.is_equal)
                        else:
                            last = dve.tensor_scalar(hot[:, u, j, :], columns,
                                                     rel_now[:, u, j:j + 1], w_now[:, u, j:j + 1],
                                                     ALU.is_equal, ALU.mult)
                    if i == (mine - 1) // QUART:
                        last.then_inc(sem("hot_done"), 1)

                if not general:
                    stage_edges(0, 0, 0, None, 0)
                    for i in range(4):
                        one_hots(i, 0, 0, iota_ps(0))
                for p in range(PASSES):
                    def add_sums(s, base, u):
                        dve.wait_ge(sem("summed"), before("summed", p, general) + s + 3)
                        dve.tensor_tensor(at(acc, base, WIN), at(acc, base, WIN), sum_ps[u][0:D, 0:WIN],
                                          ALU.add).then_inc(sem("added"), 1)
                        if p == 0:
                            dve.tensor_tensor(at(counts, base, WIN), at(counts, base, WIN),
                                              aux_ps[u][0:R65, 0:WIN], ALU.add)\
                               .then_inc(sem("counts_done"), 1)
                            dve.wait_ge(sem("counts_done"), s + 1)
                        dve.wait_ge(sem("added"), before("added", p, general) + s + 1)
                        dve.sem_inc(sem("dve_turns"), 1)

                    def type_one_hots(g):
                        dve.tensor_tensor(
                            type_hot[:, :, :], iota_type[:, :].rearrange("p (j t) -> p j t", t=R65),
                            col16(t65_bf, g).unsqueeze(2).to_broadcast([128, TILE, R65]), ALU.is_equal)\
                           .then_inc(sem("type_hot_done"), 1)

                    def count_one_hots(s, g, u):
                        dve.wait_ge(sem("summed"), before("summed", p, general) + s + 2)
                        for j in range(TILE):
                            dve.tensor_scalar(hot_bf[:, j, :], iota_ps(0), rel_now[:, u, j:j + 1],
                                              None, ALU.is_equal)
                        type_one_hots(g)

                    def start_look_up(s, g, k):
                        dve.wait_ge(sem("summed"), before("summed", p, general) + s + 2)
                        type_one_hots(g)
                        window = at(counts, k * WIN if general else g * STEP, WIN)
                        dve.tensor_copy(inv_now[:, 0, :], window).then_inc(sem("inv_parts"), 1)
                        dve.wait_ge(sem("inv_parts"), 4 * s + 1)
                        dve.tensor_tensor(inv_rest[:, :], window, inv_now[:, 0, :], ALU.subtract)\
                           .then_inc(sem("inv_parts"), 1)
                        dve.wait_ge(sem("inv_parts"), 4 * s + 2)
                        dve.tensor_copy(inv_now[:, 1, :], inv_rest[:, :]).then_inc(sem("inv_parts"), 1)
                        dve.wait_ge(sem("inv_parts"), 4 * s + 3)
                        dve.tensor_tensor(inv_now[:, 2, :], inv_rest[:, :], inv_now[:, 1, :], ALU.subtract)\
                           .then_inc(sem("inv_parts"), 1)

                    def look_up(i, s, u):
                        for j in range(QUART * i, QUART * (i + 1)):
                            if j % 2 == 0:
                                dve.wait_ge(sem("look_done"), TILE // 2 * s + j // 2 + 1)
                            last = dve.scalar_tensor_tensor(
                                out=junk[:, j % 4, :], in0=iota_win[:, :], scalar=rel_now[:, u, j:j + 1],
                                in1=tab_ps[j // 2 % 2][:, (j % 2) * WIN:(j % 2 + 1) * WIN],
                                op0=ALU.is_equal, op1=ALU.mult, accum_out=mean_now[:, j:j + 1])
                            if j % 2:
                                last.then_inc(sem("look_used"), 1)

                    def end_look_up(s, g):
                        dve.wait_ge(sem("look_used"), TILE // 2 * s + TILE // 2 + 2)
                        dve.tensor_tensor(col16(mean_w, g), col16(mean_w, g), mean_now[:, :], ALU.add)\
                           .then_inc(sem("mean_w_done"), 1)
                        dve.wait_ge(sem("mean_w_done"), s + 1)

                    def turn(s, g, k, u, n, b):
                        if general:
                            stage_edges(p, s, g, k, u)
                            for i in range(4):
                                one_hots(i, p, u, iota_ps(p))
                        elif b is not None or s == 1:
                            add_last(s, 1 - u)
                        if b is not None:
                            finish(0, b)
                        if p == 0:
                            count_one_hots(s, g, u)
                        if looks_in_turn(p, general, s):
                            start_look_up(s, g, k)
                        q, t = ahead(p, s)
                        run_ahead = not general and q < PASSES
                        if run_ahead:
                            stage_edges(q, t, t, None, 1 - u)
                        for i in range(4):
                            if run_ahead:
                                one_hots(i, q, 1 - u, iota_ps(p))
                            if b is not None and i + 1 < phases_in_turn(p, s):
                                finish(i + 1, b)
                            if looks_in_turn(p, general, s):
                                look_up(i, s, u)
                        if looks_in_turn(p, general, s):
                            end_look_up(s, g)
                        if general:
                            add_sums(s, k * WIN, u)

                    def add_last(s, u):
                        if isinstance(s, int) and s == 1:
                            dve.wait_ge(sem("cleared"), before("cleared", p, general))
                        elif p == REL:
                            dve.wait_ge(sem("conv_sum"), before("conv_sum", p, general) + s - 2)
                        else:
                            dve.wait_ge(sem("cleared"), before("cleared", p, general) + s - 2)
                        add_sums(s - 1, (s - 1) * STEP, u)

                    def clear(b):
                        dve.tensor_copy(sums_of(b), zeros[:, :]).then_inc(sem("cleared"), 1)

                    def norm(b, y):
                        dve.bn_stats(stats[:, :], y).then_inc(sem("stats"), 1)
                        dve.wait_ge(sem("stats"), before("stats", p, general) + b + 1)
                        dve.sem_inc(sem("dve_turns"), 1)
                        dve.bn_aggr(mean_var[:, :], stats[:, :]).then_inc(sem("moments"), 1)
                        dve.wait_ge(sem("std_done"), before("std_done", p, general) + b + 1)
                        dve.reciprocal(rstd[:, :], std[:, :]).then_inc(sem("rstd"), 1)
                        dve.wait_ge(sem("rstd"), before("rstd", p, general) + b + 1)
                        if p == 2:
                            dve.tensor_scalar(z_blk[:, 1, :], y, mean_var[:, 0:1], rstd[:, :],
                                              ALU.subtract, ALU.mult)
                        if p == 4:
                            dve.tensor_scalar(nm_at(x_nm, b), y, mean_var[:, 0:1], rstd[:, :],
                                              ALU.subtract, ALU.mult)
                        if p == REL:
                            dve.wait_ge(sem("stored"), before("stored", p, general) + 16 * b)
                        dve.tensor_scalar(z_blk[:, 0, :], y, mean_var[:, 0:1], rstd[:, :],
                                          ALU.subtract, ALU.mult)\
                           .then_inc(sem("rows_ready" if p == REL else "z_done"), 1)

                    def low_parts(b):
                        done = before("parts", p, general) + 3 * b
                        dve.wait_ge(sem("parts_begun"), before("parts_begun", p, general) + b + 1)
                        dve.tensor_tensor(x_rest[D:128, :], fm_a[D:128, :], x_hi_mid[D:128, :], ALU.subtract)\
                           .then_inc(sem("parts"), 1)
                        dve.wait_ge(sem("parts"), done + 1)
                        dve.tensor_copy(x_hi_mid[D:128, :], x_rest[D:128, :]).then_inc(sem("parts"), 1)
                        dve.wait_ge(sem("parts"), done + 2)
                        dve.tensor_tensor(x_hi_lo[D:128, :], x_rest[D:128, :], x_hi_mid[D:128, :], ALU.subtract)\
                           .then_inc(sem("parts"), 1)

                    def table(b, chunks):
                        if 0 in chunks:
                            dve.wait_ge(sem("stored"), before("stored", p, general) + 32 * b)
                        for c in chunks:
                            if c % 2 == 0:
                                continue
                            o, w = CHUNKS[c]
                            dve.wait_ge(sem("tab_mult"), before("tab_mult", p, general) + 9 * b + c + 1)
                            dve.tensor_copy(table_blk[0:BLK, o:o + w], tab_ps[c % 3][0:BLK, 0:w])\
                               .then_inc(sem("tab_dve"), 1)

                    def conv_start(b, source):
                        dve.tensor_copy(in_blk[:, :], cols_of(source, b)).then_inc(sem("in_done"), 1)
                        dve.wait_ge(sem("conv_mult"), before("conv_mult", p, general) + b + 1)
                        dve.tensor_tensor(y_blk[:, :], fm_a[0:D, :], sums_of(b), ALU.add)\
                           .then_inc(sem("conv_sum"), 1)

                    def finish(i, b):
                        if p in GIN:
                            if i == 0:
                                dve.tensor_tensor(in_blk[:, :], sums_of(b),
                                                  cols_of(x_fm if p == 0 else h_fm, b), ALU.add)\
                                   .then_inc(sem("in_done"), 1)
                            elif p < 2 and i == 2:
                                dve.wait_ge(sem("out_turned"), before("out_turned", p, general) + b + 1)
                                dve.wait_ge(sem("stored"), before("stored", p, general) + 16 * b)
                                dve.tensor_copy(nm_blk[:, :], nm_ps).then_inc(sem("rows_ready"), 1)
                                clear(b)
                            elif p == 2 and i == 1:
                                dve.wait_ge(sem("out_done"), before("out_done", p, general) + b + 1)
                                dve.tensor_tensor(y_blk[:, :], out_blk[:, :], cols_of(x_fm, b), ALU.add)\
                                   .then_inc(sem("y_done"), 1)
                                clear(b)
                            elif p == 2 and i == 2:
                                dve.wait_ge(sem("y_turned"), before("y_turned", p, general) + b + 1)
                                norm(b, nm_ps)
                            elif p == 2 and i == 3:
                                low_parts(b)
                            elif p == 2:
                                table(b, range(len(CHUNKS)))
                        elif p == 3:
                            if i == 0:
                                conv_start(b, x_fm)
                            elif i == 1:
                                dve.wait_ge(sem("conv_relu"), before("conv_relu", p, general) + b + 1)
                                dve.tensor_tensor(cols_of(h_fm, b), out_blk[:, :], res_blk[:, :], ALU.add)
                                dve.tensor_tensor(xblk[:, :], out_blk[:, :], res_blk[:, :], ALU.add)\
                                   .then_inc(sem("h_done"), 1)
                                clear(b)
                            elif i == 3:
                                low_parts(b)
                            elif i == 4:
                                table(b, range(len(CHUNKS)))
                        elif p == 4:
                            if i == 0:
                                conv_start(b, h_fm)
                            elif i == 1:
                                dve.wait_ge(sem("conv_relu"), before("conv_relu", p, general) + b + 1)
                                dve.tensor_tensor(res_blk[:, :], out_blk[:, :], res_blk[:, :], ALU.add)\
                                   .then_inc(sem("h2_done"), 1)
                                clear(b)
                                dve.wait_ge(sem("h2_done"), b + 1)
                                dve.tensor_tensor(y_blk[:, :], res_blk[:, :], cols_of(x_fm, b), ALU.add)\
                                   .then_inc(sem("y_done"), 1)
                            elif i == 2:
                                dve.wait_ge(sem("y_turned"), before("y_turned", p, general) + b + 1)
                                norm(b, nm_ps)
                            elif i == 4:
                                dve.wait_ge(sem("gcn_mult"), b + 1)
                                dve.tensor_scalar(nm_at(hws_nm, b), nm_ps, at(dinv, b), None, ALU.mult)
                                dve.wait_ge(sem("stored"), before("stored", p, general) + 16 * b)
                                dve.tensor_scalar(nm_blk[:, :], nm_ps, at(dinv, b), None, ALU.mult)\
                                   .then_inc(sem("rows_ready"), 1)
                        elif p == GCN:
                            if i > 0:
                                return
                            dve.tensor_copy(in_blk[:, :], sums_of(b)).then_inc(sem("in_done"), 1)
                            dve.wait_ge(sem("sum_turned"), b + 1)
                            dve.tensor_tensor(y_nm[:, :], nm_ps, nm_at(hws_nm, b), ALU.add)\
                               .then_inc(sem("gcn_steps"), 1)
                            clear(b)
                            dve.wait_ge(sem("gcn_steps"), 4 * b + 1)
                            dve.scalar_tensor_tensor(out=y_nm[:, :], in0=y_nm[:, :], scalar=at(dinv, b),
                                                     in1=gcn_b[:, :], op0=ALU.mult, op1=ALU.add)\
                               .then_inc(sem("gcn_steps"), 1)
                            dve.wait_ge(sem("gcn_steps"), 4 * b + 2)
                            dve.tensor_scalar(neg_nm[:, :], y_nm[:, :], 0.0, prelu_a[:, :], ALU.min, ALU.mult)\
                               .then_inc(sem("gcn_steps"), 1)
                            dve.wait_ge(sem("gcn_steps"), 4 * b + 3)
                            dve.scalar_tensor_tensor(out=y_nm[:, :], in0=y_nm[:, :], scalar=0.0,
                                                     in1=neg_nm[:, :], op0=ALU.max, op1=ALU.add)\
                               .then_inc(sem("gcn_steps"), 1)
                            dve.wait_ge(sem("gcn_steps"), 4 * b + 4)
                            dve.tensor_tensor(y_nm[:, :], y_nm[:, :], nm_at(x_nm, b), ALU.add)\
                               .then_inc(sem("y_done"), 1)
                            dve.wait_ge(sem("y_done"), before("y_done", p, general) + b + 1)
                            norm(b, y_nm[:, :])
                        else:
                            if i == 0:
                                conv_start(b, h_fm)
                            elif i == 1:
                                dve.wait_ge(sem("conv_relu"), before("conv_relu", p, general) + b + 1)
                                dve.tensor_tensor(res_blk[:, :], out_blk[:, :], cols_of(h_fm, b), ALU.add)\
                                   .then_inc(sem("h_sum"), 1)
                                dve.wait_ge(sem("h_sum"), b + 1)
                                dve.tensor_tensor(y_blk[:, :], res_blk[:, :], cols_of(x_fm, b), ALU.add)\
                                   .then_inc(sem("y_done"), 1)
                            elif i == 2:
                                dve.wait_ge(sem("y_turned"), before("y_turned", p, general) + b + 1)
                                norm(b, nm_ps)

                    def wait_for_weights():
                        dve.wait_ge(sem("x_fm_done"), XBANKS)
                        dve.wait_ge(sem("weights_in"), WEIGHTS)

                    def split_w():
                        layer = p - 2
                        dve.wait_ge(sem("w_high"), layer + 1)
                        dve.tensor_tensor(table_blk[:, :], table_blk[:, :], w_hi[:, :], ALU.subtract)\
                           .then_inc(sem("w_rest"), 1)
                        dve.wait_ge(sem("w_middle"), layer + 1)
                        dve.tensor_tensor(w_lo_hi[0:D, :], table_blk[0:D, :], w_mid[0:D, :], ALU.subtract)\
                           .then_inc(sem("w_split"), 1)

                    if p == 2:
                        dve.tensor_copy(iota_ps(2), iota_win[:, :]).then_inc(sem("fills"), 1)
                        dve.wait_ge(sem("fills"), 6)
                    if general and p > 0:
                        dve.wait_ge(sem("cleared"), before("cleared", p, general))
                    schedule(dve, general, turn, finish,
                             {0: wait_for_weights, 2: split_w, 3: split_w}.get(p))
                    if not general:
                        add_last(NG, 1)
                        finish_last(p, finish, table)
                        if p == 1:
                            start_look_up(NG - 1, NG - 1, None)
                            for i in range(4):
                                look_up(i, NG - 1, 1)
                            end_look_up(NG - 1, NG - 1)
                    if p == 0:
                        dve.wait_ge(sem("degree_root"), 1)
                        dve.reciprocal(dinv[:, :], dinv[:, :]).then_inc(sem("dinv_done"), 1)
                        dve.tensor_scalar(counts[:, :], counts[:, :], 1.0, None, ALU.max)\
                           .then_inc(sem("counts_max"), 1)
                        dve.wait_ge(sem("counts_max"), 1)
                        dve.reciprocal(counts[:, :], counts[:, :]).then_inc(sem("inverse_done"), 1)
                        dve.wait_ge(sem("inverse_done"), 1)

            by_branch(dve, run)


_INS = ["x", "src", "dst", "edge_type_65", "edge_type_8", "edge_weight",
        "L0_gnn_w11", "L0_gnn_b11", "L0_gnn_w12", "L0_gnn_b12", "L0_gnn_w21", "L0_gnn_b21",
        "L0_gnn_w22", "L0_gnn_b22", "L0_gnn_w31", "L0_gnn_b31", "L0_gnn_w32", "L0_gnn_b32",
        "L1_gnn_W", "L1_gnn_root", "L1_gnn_bias", "L1_gnn_res_W", "L1_gnn_res_b",
        "L2_gnn_W", "L2_gnn_b", "L2_gnn_prelu_a",
        "L3_gnn_W_enc", "L3_gnn_b_enc", "L3_gnn_W_rel", "L3_gnn_W_self", "L3_gnn_bias"]


def kernel(**inputs):
    import numpy as _np
    import concourse.bacc as _bacc
    from concourse import mybir as _mybir
    from concourse.bass_utils import run_bass_kernel_spmd as _run

    nc = _bacc.Bacc("TRN2", target_bir_lowering=False, num_devices=1)
    arrays, args = {}, {}
    for name in _INS:
        a = _np.ascontiguousarray(inputs[name])
        arrays[f"in_{name}_dram"] = a
        args[name] = nc.dram_tensor(f"in_{name}_dram", a.shape, _mybir.dt.from_np(a.dtype),
                                    kind="ExternalInput").ap()
    n, d = inputs["x"].shape
    sizes = {"h1": n, "h2": n, "hw": n, "t8": n * 8, "t65a": n * 65, "t65b": n * 65}
    scratch = {name: nc.dram_tensor(f"table_{name}", (r, d), F32, kind="Internal").ap()
               for name, r in sizes.items()}
    out = nc.dram_tensor("out_0_dram", (n, d), _mybir.dt.float32, kind="ExternalOutput").ap()
    bass_gnn(nc, args, out, scratch)
    r = _run(nc, [arrays], core_ids=[0])
    return r.results[0]["out_0_dram"]
```
